# Optimizing a Trainium2 kernel written in Bass

```python
import numpy as np
import jax
import jax.numpy as jnp

def _softmax(x, axis=-1):
    return jax.nn.softmax(x, axis=axis)

def _gelu(x):
    return jax.nn.gelu(x, approximate=True)

def _silu(x):
    return jax.nn.silu(x)

def _sigmoid(x):
    return jax.nn.sigmoid(x)

def _layernorm(x, axis=-1, eps=1e-05):
    m = jnp.mean(x, axis=axis, keepdims=True)
    v = jnp.var(x, axis=axis, keepdims=True)
    return (x - m) / jnp.sqrt(v + eps)

def _scatter_add(tgt, idx, src, axis=0):
    return tgt.at[idx].add(src)

def _segment_sum(src, seg, n):
    return jax.ops.segment_sum(src, seg, n)
kernel_name = 'mk_xattn_ffn_d1_seqx_r4_440933'

def setup_inputs(seed: int=0):
    np.random.seed(seed)
    _w = jnp.asarray

    def _rec_inputs():
        import jax
        import jax.numpy as jnp
        _rk = jax.random.key(seed)
        x = -0.0002928 + 1 * jax.random.normal(jax.random.fold_in(_rk, 1), (8, 512, 256), jnp.float32)
        _lenS = 512 - jax.random.randint(jax.random.fold_in(_rk, 7), (8,), 0, max(1, 512 // 4) + 1, jnp.int32)
        _lenS2 = 512 - jax.random.randint(jax.random.fold_in(_rk, 8), (8,), 0, max(1, 512 // 4) + 1, jnp.int32)
        _ctx_1024P = jax.random.normal(jax.random.fold_in(_rk, 11), (8, 16, 256), jnp.float32)
        _ctx_1024c = jax.random.dirichlet(jax.random.fold_in(_rk, 511), 0.3 * jnp.ones((16,), jnp.float32), (8, 512))
        _ctx_1024t = jnp.einsum('bsk,bkd->bsd', _ctx_1024c, _ctx_1024P)
        _ctx_1024t = _ctx_1024t * jax.lax.rsqrt(jnp.mean(jnp.square(_ctx_1024t)) + 1e-12) * 0.953939
        ctx_1024 = -1.39393e-06 + 0.999914 * (_ctx_1024t + 0.3 * jax.random.normal(jax.random.fold_in(_rk, 611), (8, 512, 256), jnp.float32))
        return (x, ctx_1024)
    x, ctx_1024 = _rec_inputs()

    def _L0_xattn_setup():
        import jax, jax.numpy as jnp
        import numpy as np
        HEADS = 16
        key = jax.random.key(seed)
        k1, k2, k3, k4 = jax.random.split(key, 4)
        B, T, S, W = (2, 512, 512, 256)
        x = jax.random.normal(k1, (B, T, W), dtype=jnp.float32)
        cond_k = jax.random.normal(k2, (B, S, W), dtype=jnp.float32)
        cond_v = jax.random.normal(k3, (B, S, W), dtype=jnp.float32)
        w_proj = jax.random.normal(k4, (W, W), dtype=jnp.float32) * 0.02
        b_proj = jnp.zeros((W,), dtype=jnp.float32)
        return {'x': x, 'cond_k': cond_k, 'cond_v': cond_v, 'w_proj': w_proj, 'b_proj': b_proj}
    _L0_xattn_all = _L0_xattn_setup()
    _L0_xattn_in = {k: v for k, v in _L0_xattn_all.items() if k in ('w_proj', 'b_proj')}
    del _L0_xattn_all

    def _L0_ffn_setup():
        import jax, jax.numpy as jnp
        import numpy as np
        EMB_DIM = 256
        HIDDEN = int(2 / 3 * 4 * EMB_DIM)
        NUM_EXPERTS = 8
        TOP_K = 2
        B, S = (4, 256)
        key = jax.random.key(seed)
        ks = jax.random.split(key, 5)
        sc = 1.0 / np.sqrt(EMB_DIM)
        sh = 1.0 / np.sqrt(HIDDEN)
        return {'x': jax.random.normal(ks[0], (B, S, EMB_DIM), dtype=jnp.float32), 'Wg': jax.random.normal(ks[1], (NUM_EXPERTS, EMB_DIM), dtype=jnp.float32) * sc, 'W1': jax.random.normal(ks[2], (NUM_EXPERTS, HIDDEN, EMB_DIM), dtype=jnp.float32) * sc, 'W2': jax.random.normal(ks[3], (NUM_EXPERTS, HIDDEN, EMB_DIM), dtype=jnp.float32) * sc, 'W3': jax.random.normal(ks[4], (NUM_EXPERTS, EMB_DIM, HIDDEN), dtype=jnp.float32) * sh}
    _L0_ffn_all = _L0_ffn_setup()
    _L0_ffn_in = {k: v for k, v in _L0_ffn_all.items() if k in ('Wg', 'W1', 'W2', 'W3')}
    del _L0_ffn_all
    return {'x': x, 'ctx_1024': ctx_1024, 'L0_xattn_w_proj': _L0_xattn_in['w_proj'], 'L0_xattn_b_proj': _L0_xattn_in['b_proj'], 'L0_ffn_Wg': _L0_ffn_in['Wg'], 'L0_ffn_W1': _L0_ffn_in['W1'], 'L0_ffn_W2': _L0_ffn_in['W2'], 'L0_ffn_W3': _L0_ffn_in['W3']}

def reference(x, ctx_1024, L0_xattn_w_proj, L0_xattn_b_proj, L0_ffn_Wg, L0_ffn_W1, L0_ffn_W2, L0_ffn_W3):
    import jax
    import jax.numpy as jnp

    def _L0_xattn_ref(x, cond_k, cond_v, w_proj, b_proj):
        import jax, jax.numpy as jnp
        import numpy as np
        HEADS = 16
        B, T, W = x.shape
        S = cond_k.shape[1]
        H = HEADS
        d = W // H
        scale = 1.0 / jnp.sqrt(jnp.sqrt(jnp.float32(d)))
        q = x.reshape(B, T, H, d) * scale
        k = cond_k.reshape(B, S, H, d) * scale
        v = cond_v.reshape(B, S, H, d)
        scores = jnp.einsum('bthd,bshd->bhts', q, k)
        w = jax.nn.softmax(scores.astype(jnp.float32), axis=-1).astype(scores.dtype)
        out = jnp.einsum('bhts,bshd->bthd', w, v).reshape(B, T, W)
        return out @ w_proj.T + b_proj

    def _L0_ffn_ref(x, Wg, W1, W2, W3):
        import jax, jax.numpy as jnp
        import numpy as np
        EMB_DIM = 256
        HIDDEN = int(2 / 3 * 4 * EMB_DIM)
        NUM_EXPERTS = 8
        TOP_K = 2
        B, S = (4, 256)
        gate_logits = jnp.einsum('bsd,ed->bse', x, Wg)
        top_v, top_i = jax.lax.top_k(gate_logits, TOP_K)
        mask = jnp.any(top_i[..., :, None] == jnp.arange(NUM_EXPERTS), axis=-2)
        sparse_logits = jnp.where(mask, gate_logits, -jnp.inf)
        gating = jax.nn.softmax(sparse_logits, axis=-1)
        h1 = jnp.einsum('bsd,ehd->bseh', x, W1)
        h2 = jnp.einsum('bsd,ehd->bseh', x, W2)
        hidden = jax.nn.silu(h1) * h2
        expert_out = jnp.einsum('bseh,edh->bsed', hidden, W3)
        return jnp.einsum('bsed,bse->bsd', expert_out, gating)
    x = x + _L0_xattn_ref(_layernorm(x, axis=-1), ctx_1024, ctx_1024, L0_xattn_w_proj, L0_xattn_b_proj)
    x = x + _L0_ffn_ref(_layernorm(x, axis=-1), L0_ffn_Wg, L0_ffn_W1, L0_ffn_W2, L0_ffn_W3)
    return x

_drawn_inputs = setup_inputs


def setup_inputs(seed=0):
    import zlib

    import numpy as np

    out = dict(_drawn_inputs(seed))
    spreads = {'L0_xattn_b_proj': (0.0, 0.1)}
    factors = {}
    for name, (base, spread) in spreads.items():
        noise = np.random.default_rng([zlib.crc32(name.encode()), seed]).standard_normal(out[name].shape)
        drawn = base * np.exp(spread * noise) if base else spread * noise
        out[name] = jnp.asarray(drawn.astype(out[name].dtype))
    for name, factor in factors.items():
        out[name] = (out[name] * factor).astype(out[name].dtype)
    return out
```

```python
from contextlib import ExitStack

import concourse.bass as bass
from concourse import mybir

ALU = mybir.AluOpType
ACT = mybir.ActivationFunctionType
AX = mybir.AxisListType
F32 = mybir.dt.float32
F16 = mybir.dt.float16
I32 = mybir.dt.int32
U32 = mybir.dt.uint32

P = 128
B, T, W = 8, 512, 256
H, D = 16, 16
NT = T // P
PAIRS = H // 2
STACK = 3 * D
QROWS = STACK + 1
E, HID = 8, 682
HC = 6
HP = (HID + HC - 1) // HC
TOKENS = B * T
SLOTS = 256
SUB = SLOTS // P
FFN_TILES = 2 * TOKENS // SLOTS + E - 1
REGION = TOKENS + SLOTS
ROW = W + 2
WSCALE = 256.0
EPS = 1e-5

C_ID = 0
C_U = C_ID + P
C_LT = C_U + P
C_LE = C_LT + E * E
C_TRASH = C_LE + E * E
C_TOK = C_TRASH + SUB
C_REG = C_TOK + NT
C_CNT = C_REG + E
NCNT = TOKENS // SLOTS
C_K = C_CNT + NCNT
C_KS = C_K + FFN_TILES
C_E = C_KS + FFN_TILES
C_ROW = C_E + E
C_EPS = C_ROW + 1
C_POW = C_EPS + 1
NCONST = C_POW + 1


def constants():
    import numpy as np

    c = np.zeros((P, NCONST), np.float32)
    p = np.arange(P)
    c[:, C_ID:C_ID + P] = np.eye(P)
    c[:, C_U:C_U + P] = p[:, None] < p[None, :]
    e = np.arange(E)
    c[:, C_LT:C_LT + E * E] = (e[None, :] < e[:, None]).reshape(-1)
    c[:, C_LE:C_LE + E * E] = (e[None, :] <= e[:, None]).reshape(-1)
    c[:, C_TRASH:C_TRASH + SUB] = TOKENS + p[:, None] + P * np.arange(SUB)
    c[:, C_TOK:C_TOK + NT] = p[:, None] + P * np.arange(NT)
    c[:, C_REG:C_REG + E] = REGION * e
    c[:, C_CNT:C_CNT + NCNT] = SLOTS * np.arange(NCNT)
    c[:, C_K:C_K + FFN_TILES] = np.arange(FFN_TILES)
    c[:, C_KS:C_KS + FFN_TILES] = SLOTS * np.arange(FFN_TILES) - E * REGION
    c[:, C_E:C_E + E] = e
    c[:, C_ROW] = p % 64 == STACK
    c[:, C_EPS] = EPS
    c[:, C_POW] = -0.5
    return c


MISC = [
    (0, "max", 3, 0), (1, "heads", 2, -1), (2, "prefix", 0, -2),
    (4, "max", 0, 1), (5, "heads", 3, -1), (6, "turn", 0, -1), (6, "turn", 1, -1),
    (7, "project", 0, -1), (8, "max", 1, 1), (8, "project", 1, -1), (9, "heads", 0, 0),
    (10, "turn_q", 0, 2), (11, "turn_q", 1, 2), (12, "max", 2, 1), (12, "turn_z", 0, -1),
    (13, "heads", 1, 0), (13, "turn_z", 1, -1), (14, "logits", 0, -1), (15, "turn_l", 0, -1),
]
FIRST, LAST = -2, B + 1
LOOP = (2, B - 2)


def active(lag, it):
    return 0 <= it + lag < B


def misc_before(it):
    return sum(active(lag, i) for i in range(FIRST, it) for _, _, _, lag in MISC)


class Iteration:

    def __init__(self, it, kind):
        self.it, self.kind = it, kind

    def has(self, lag):
        return active(lag, self.kind)

    def par(self, lag=0):
        return (self.kind + lag) % 2

    def misc(self, slot):
        before = misc_before(self.kind)
        if not isinstance(self.it, int):
            before = misc_before(LOOP[0]) + len(MISC) * (self.it - LOOP[0])
        n, out = 0, []
        for s, name, i, lag in MISC:
            if active(lag, self.kind):
                if s == slot:
                    out.append((before + n, name, i, lag))
                n += 1
        return out

    def use(self, lag, name, i):
        n = [k for k, e in enumerate(MISC) if e[1] == name and e[2] == i and e[3] in (lag, lag + 1)][0]
        delta = lag - MISC[n][3]
        if isinstance(self.it, int):
            k = self.kind + delta
            return misc_before(k) + sum(active(e[3], k) for e in MISC[:n])
        assert delta == 0 or n > 2
        return misc_before(LOOP[0]) + len(MISC) * (self.it - LOOP[0] + delta) + n


def hold(eng, passed):
    eng.sem_inc(passed, 1)


def at(b):
    return slice(b, b + 1) if isinstance(b, int) else bass.ds(b, 1)


def iterations(eng, body):
    for it in range(FIRST, LOOP[0]):
        body(Iteration(it, it))
    with eng.Fori(0, (LOOP[1] - LOOP[0]) // 2) as i:
        for par in range(2):
            body(Iteration(i * 2 + (LOOP[0] + par), LOOP[0] + par))
    for it in range(LOOP[1], LAST + 1):
        body(Iteration(it, it))


def ffn_tiles(eng, body):
    for k in range(2):
        body(k, 0, k, k)
    turns = (FFN_TILES - 3) // 2
    with eng.Fori(0, turns) as i:
        for par in range(2):
            body(i * 2 + (2 + par), i + 1, par, 2 + par)
    for k in range(2 + 2 * turns, FFN_TILES):
        body(k, k // 2, k % 2, k)


def ge(eng, sem, value):
    if not isinstance(value, int) or value > 0:
        eng.wait_ge(sem, value)


class Chain:

    def __init__(self, sem, per):
        self.sem, self.per = sem, per

    def start(self, b):
        self.b, self.n = b, 0

    def step(self, ins):
        self.n += 1
        ins.then_inc(self.sem, 1)

    def wait(self, eng):
        eng.wait_ge(self.sem, self.b * self.per + self.n)


PREP_STAT, PREP_QN, PREP_QL, PREP_KL = 8, 12, 13, 14
K_PREP = PREP_KL
LN2_STAT, LN2_Z, LN2_ZL = 8, 12, 13
K_LN2 = LN2_ZL
K_ROUTE = 27
ROUTE_SEL, ROUTE_D = 8, 13


def build(nc, xq_l, x_l, v_l, kT_l, wp_l, bias, wg_l, w12_l, w3_l, const, out):
    ctx = ExitStack()
    with ctx:
        def sb(name, shape, dt=F32):
            return ctx.enter_context(nc.sbuf_tensor(name, shape, dt))

        def sem(name):
            return ctx.enter_context(nc.semaphore(name))

        q_dram = nc.dram_tensor("q_parts", (2, 2, PAIRS, QROWS, T), F16, kind="Internal").ap()
        k_dram = nc.dram_tensor("k_parts", (2, 2, PAIRS, STACK, T), F16, kind="Internal").ap()
        z_dram = nc.dram_tensor("slots", ((E + 1) * REGION, ROW), F32, kind="Internal").ap()
        w12_dram = nc.dram_tensor("w12_parts", (E, P, 2, 2, 2 * HC * HP), F16, kind="Internal").ap()
        w3_dram = nc.dram_tensor("w3_parts", (E, HP, 2, HC * W), F16, kind="Internal").ap()

        con = sb("con", [P, NCONST])
        ident = con[:, C_ID:C_ID + P]
        ident16 = sb("ident16", [P, P], F16)
        upper16 = sb("upper16", [P, P], F16)
        ones16 = sb("ones16", [P, P], F16)
        scale_w = sb("scale_w", [P, 1])
        bias_sb = sb("bias_sb", [P, W])
        wp_sb = sb("wp_sb", [P, 2, W])
        wg_sb = sb("wg_sb", [P, 2, E])
        fill = sb("fill", [P, SUB, ROW])
        run = sb("run", [P, E])

        att = ExitStack()

        def sa(name, shape, dt=F32):
            return att.enter_context(nc.sbuf_tensor(name, shape, dt))

        x_in = sa("x_in", [P, NT, W])
        kt_in = sa("kt_in", [P, 2, T])
        v_in = sa("v_in", [P, NT, W])
        q_stack = [sa(f"q_stack{i}", [P, H, T], F16) for i in range(2)]
        k_stack = [sa(f"k_stack{i}", [P, PAIRS, T], F16) for i in range(2)]
        v_ext = [sa(f"v_ext{i}", [P, NT, H, 32]) for i in range(2)]
        probs = [sa(f"probs{i}", [P, 4, NT, T]) for i in range(2)]
        heads = [sa(f"heads{i}", [P, T]) for i in range(2)]
        stats = sa("stats", [P, NT, 6])
        mv = sa("mv", [P, NT, 2])
        rstd = sa("rstd", [P, NT])
        q16 = [sa(f"q16_{i}", [P, NT, W], F16) for i in range(2)]
        qt16 = [sa(f"qt16_{i}", [P, 2, T], F16) for i in range(2)]
        k16 = [sa(f"k16_{i}", [P, 2, T], F16) for i in range(2)]
        mx = [sa(f"mx{i}", [P, NT, H]) for i in range(2)]
        neg_max = sa("neg_max", [P, NT, 4], F16)
        max_row = [sa(f"max_row{i}", [4, T], F16) for i in range(2)]
        recip = sa("recip", [P, NT, 4])
        o_norm = sa("o_norm", [P, NT, W])
        o_t = sa("o_t", [P, 2, T])
        x_res = sa("x_res", [P, NT, W])
        x2 = sa("x2", [P, NT, W])
        stats2 = sa("stats2", [P, NT, 6])
        mv2 = sa("mv2", [P, NT, 2])
        rstd2 = sa("rstd2", [P, NT])
        z_row = [sa(f"z_row{i}", [P, NT, ROW]) for i in range(2)]
        logit_t = sa("logit_t", [E, T])
        logit = sa("logit", [P, NT, E])
        cmp1 = sa("cmp1", [P, NT, E * E], F16)
        cmp2 = sa("cmp2", [P, NT, E * E], F16)
        rank = sa("rank", [P, NT * E])
        hot = [sa(f"hot{i}", [P, NT * E]) for i in range(2)]
        sel16 = sa("sel16", [P, NT * E], F16)
        pick = sa("pick", [P, NT * E])
        val = [sa(f"val{i}", [P, NT]) for i in range(2)]
        diff = sa("diff", [P, NT])
        ediff = sa("ediff", [P, NT])
        den = sa("den", [P, NT])
        gate = [sa(f"gate{i}", [P, NT]) for i in range(2)]
        pos = sa("pos", [P, NT * E])
        slot_f = sa("slot_f", [P, 2, NT])
        slot_u = sa("slot_u", [P, 2, NT], U32)
        tok = sa("tok", [P, NT])
        w_in = sa("w_in", [P, HC * W])
        w_hi = sa("w_hi", [P, HC * W], F16)
        w_lo = sa("w_lo", [P, HC * W], F16)

        ps = ctx.enter_context(nc.psum_tensor("ps", [P, 8, T], F32))
        max_bank = [ps[:, 0, :], ps[:, 1, :]]
        exp_bank = [ps[:, 2:4, :], ps[:, 4:6, :]]
        pv_bank = ps[:, 6, :]
        misc_bank = ps[:, 7, :]
        misc16 = misc_bank.bitcast(F16)

        s_con = sem("s_con")
        s_cst = sem("s_cst")
        s_zero = sem("s_zero")
        s_zq = sem("s_zq")
        s_xin, s_kin, s_vin, s_xres_ld = sem("s_xin"), sem("s_kin"), sem("s_vin"), sem("s_xres_ld")
        s_qh, s_kh = sem("s_qh"), sem("s_kh")
        s_qd, s_kd = sem("s_qd"), sem("s_kd")
        s_stk = [sem(f"s_stk{g}") for g in range(4)]
        s_mrow = [sem(f"s_mrow{g}") for g in range(4)]
        s_a = sem("s_a")
        s_red = sem("s_red")
        s_neg = sem("s_neg")
        s_b = sem("s_b")
        s_exp = sem("s_exp")
        s_vx = sem("s_vx")
        s_pv = sem("s_pv")
        s_hd = sem("s_hd")
        s_mw, s_mr = sem("s_mw"), sem("s_mr")
        s_rec = sem("s_rec")
        s_xres = sem("s_xres")
        s_rstd, s_rstd2 = sem("s_rstd"), sem("s_rstd2")
        s_x2st = sem("s_x2st")
        s_zh = sem("s_zh")
        s_zcp = sem("s_zcp")
        s_ed = sem("s_ed")
        s_sc = sem("s_sc")
        s_wld, s_wop, s_wst = sem("s_wld"), sem("s_wop"), sem("s_wst")
        s_prep, s_ln2, s_route = sem("s_prep"), sem("s_ln2"), sem("s_route")
        prep = Chain(s_prep, K_PREP)
        ln2 = Chain(s_ln2, K_LN2)
        route = Chain(s_route, K_ROUTE)
        s_pad = sem("s_pad")
        s_held = [sem(f"s_held{i}") for i in range(4)]
        s_tab = sem("s_tab")

        out_v = out[0:TOKENS, :].rearrange("(b i p) c -> b p i c", p=P, i=NT)

        attention = ExitStack()
        block = attention.enter_context(nc.Block())

        @block.sync
        def _(sp):
            sp.dma_start(con[:, :], const).then_inc(s_con, 16)
            sp.dma_start(bias_sb[:, :], bias.partition_broadcast(P)).then_inc(s_con, 16)
            sp.dma_start(wp_sb[:, :, :], wp_l).then_inc(s_con, 16)
            sp.dma_start(wg_sb[:, :, :], wg_l).then_inc(s_con, 16)
            sp.wait_ge(s_zero, 1)
            for r in range(2):
                for par in range(2):
                    sp.dma_start(q_dram[r, par, :, STACK, :], k_stack[0][0:PAIRS, 0, :]).then_inc(s_zq, 16)
            sp.wait_ge(s_cst, 4)
            sp.dma_start(out[TOKENS:TOKENS + SLOTS, :].rearrange("(s p) c -> p s c", p=P),
                         fill[:, :, 0:W]).then_inc(s_pad, 16)
            sp.dma_start(z_dram[E * REGION:E * REGION + SLOTS, :].rearrange("(s p) c -> p s c", p=P),
                         fill[:, :, :]).then_inc(s_pad, 16)

            def load_stacks(it, lag, g):
                b, r = it.it + lag, it.par(lag)
                if g == 0:
                    sp.wait_ge(s_kd, (b + 1) * 96)
                    sp.wait_ge(s_qd, (b + 1) * 96)
                if it.kind + lag >= 2:
                    sp.wait_ge(s_b, (b - 2) * 32 + 8 * (g + 1))
                for par in range(2):
                    lo = 64 * par
                    sp.dma_start(k_stack[r][lo:lo + STACK, 2 * g:2 * g + 2, :],
                                 k_dram[r, par, 2 * g:2 * g + 2].rearrange("a r t -> r a t")).then_inc(s_stk[g], 16)
                    sp.dma_start(q_stack[r][lo:lo + QROWS, 4 * g + par:4 * g + 4:2, :],
                                 q_dram[r, par, 2 * g:2 * g + 2].rearrange("a r t -> r a t")).then_inc(s_stk[g], 16)

            def load_max(it, lag, g):
                b, r = it.it + lag, it.par(lag)
                sp.wait_ge(s_mr, it.use(lag, "max", g) + 1)
                for n in range(4):
                    par, pl = n // 2, n % 2
                    row = 64 * par + STACK
                    sp.dma_start(q_stack[r][row:row + 1, 4 * g + 2 * pl + par, :],
                                 max_row[g % 2][n:n + 1, :]).then_inc(s_mrow[g], 16)

            def body(it):
                if it.has(2):
                    b = it.it + 2
                    if it.kind + 2 >= 1:
                        sp.wait_ge(s_prep, b * K_PREP)
                        sp.wait_ge(s_kh, b)
                    sp.dma_start(x_in[:, :, :], xq_l[at(b)].squeeze(0)).then_inc(s_xin, 16)
                    sp.dma_start(kt_in[:, :, :], kT_l[at(b)].squeeze(0)).then_inc(s_kin, 16)
                if it.has(1):
                    b = it.it + 1
                    ge(sp, s_vx, b)
                    sp.dma_start(v_in[:, :, :], v_l[at(b)].squeeze(0)).then_inc(s_vin, 16)
                if it.has(-1):
                    b = it.it - 1
                    if it.kind - 1 >= 1:
                        sp.wait_ge(s_mr, it.use(-2, "project", 1) + 1)
                    sp.dma_start(x_res[:, :, :], x_l[at(b)].squeeze(0)).then_inc(s_xres_ld, 16)
                if it.has(1):
                    load_stacks(it, 1, 3)
                if it.has(0):
                    load_max(it, 0, 3)
                if it.has(2):
                    b, r = it.it + 2, it.par(2)
                    sp.wait_ge(s_kh, b + 1)
                    hold(sp, s_held[3])
                    sp.wait_ge(s_prep, b * K_PREP + PREP_KL)
                    for j, part in enumerate((0, 1, 0)):
                        for par in range(2):
                            sp.dma_start(k_dram[r, par, :, j * D:(j + 1) * D, :],
                                         k16[part][:, par, :]).then_inc(s_kd, 16)
                if it.has(1):
                    load_max(it, 1, 0)
                    load_max(it, 1, 1)
                if it.has(-1):
                    b = it.it - 1
                    sp.wait_ge(s_mr, it.use(-1, "project", 1) + 1)
                    hold(sp, s_held[3])
                    if it.kind - 1 >= 1:
                        sp.wait_ge(s_x2st, b * 16)
                    sp.dma_start(out_v[at(b)].squeeze(0), x2[:, :, :]).then_inc(s_x2st, 16)
                if it.has(2):
                    b, r = it.it + 2, it.par(2)
                    sp.wait_ge(s_mr, it.use(2, "turn_q", 1) + 1)
                    if it.kind == FIRST:
                        sp.wait_ge(s_zq, 64)
                    for j, part in enumerate((0, 0, 1)):
                        for par in range(2):
                            sp.dma_start(q_dram[r, par, :, j * D:(j + 1) * D, :],
                                         qt16[part][:, par, :]).then_inc(s_qd, 16)
                    for g in range(3):
                        load_stacks(it, 2, g)
                if it.has(1):
                    load_max(it, 1, 2)

            iterations(sp, body)
            sp.wait_ge(s_x2st, 16 * B)
            sp.wait_ge(s_pad, 32)

        @block.gpsimd
        def _(pool):
            pool.wait_ge(s_con, 64)
            for i in range(2):
                nc.gpsimd.memset(k_stack[i][:, :, :].bitcast(F32), 0.0).then_inc(s_zero, 1)
            for i in range(2):
                nc.gpsimd.memset(v_ext[i][:, :, :, :], 0.0).then_inc(s_zero, 1)
            nc.gpsimd.memset(scale_w[:, :], WSCALE).then_inc(s_zero, 1)
            nc.gpsimd.memset(ones16[:, :], 1.0).then_inc(s_zero, 1)
            pool.wait_ge(s_zero, 6)
            for i in range(2):
                nc.gpsimd.memset(v_ext[i][:, :, :, D:D + 1], 1.0).then_inc(s_zero, 1)
            pool.wait_ge(s_zero, 8)

            def inverse_root(agg, rs, done, b):
                nc.gpsimd.tensor_tensor(rs[:, :], agg[:, :, 1], con[:, C_EPS:C_EPS + 1].to_broadcast([P, NT]),
                                        ALU.add).then_inc(done, 1)
                pool.wait_ge(done, b * 2 + 1)
                nc.gpsimd.tensor_tensor(rs[:, :], rs[:, :], con[:, C_POW:C_POW + 1].to_broadcast([P, NT]),
                                        ALU.pow).then_inc(done, 1)

            def split_weights(e, kind, c):
                n = e * 3 + c
                rows, size = (P, 2 * HC * HP) if c < 2 else (HP, HC * W)
                src = w12_l[at(e), c].squeeze(0) if c < 2 else w3_l[at(e)].squeeze(0)
                dst = w12_dram[at(e), :, c] if c < 2 else w3_dram[at(e)]
                x, hi, lo = w_in[0:rows, 0:size], w_hi[0:rows, 0:size], w_lo[0:rows, 0:size]
                by = scale_w[0:rows, 0:1].to_broadcast([rows, size])
                if kind or c:
                    pool.wait_ge(s_wop, n * 3)
                pool.dma_start(x, src).then_inc(s_wld, 16)
                pool.wait_ge(s_wld, (n + 1) * 16)
                if kind or c:
                    pool.wait_ge(s_wst, n * 32)
                nc.gpsimd.tensor_tensor(hi, x, by, ALU.mult).then_inc(s_wop, 1)
                pool.wait_ge(s_wop, n * 3 + 1)
                nc.gpsimd.tensor_tensor(x, x, by, ALU.mult).then_inc(s_wop, 1)
                pool.wait_ge(s_wop, n * 3 + 2)
                nc.gpsimd.tensor_tensor(lo, x, hi, ALU.subtract).then_inc(s_wop, 1)
                pool.wait_ge(s_wop, n * 3 + 3)
                for part, y in enumerate((hi, lo)):
                    pool.dma_start(dst[:, :, part].squeeze(0), y).then_inc(s_wst, 16)

            def body(it):
                if it.has(-1):
                    b, r = it.it - 1, it.par(-1)
                    pool.wait_ge(s_xres_ld, (b + 1) * 16)
                    xb = x_res[:, :, :]
                    nc.gpsimd.tensor_tensor(xb, xb, bias_sb[:, :].unsqueeze(1).broadcast_to([P, NT, W]),
                                            ALU.add).then_inc(s_xres, 1)
                if it.has(1):
                    b, r = it.it + 1, it.par(1)
                    pool.wait_ge(s_vin, (b + 1) * 16)
                    if it.kind + 1 >= 2:
                        pool.wait_ge(s_pv, (b - 1) * 4)
                    hold(pool, s_held[2])
                    nc.gpsimd.tensor_copy(v_ext[r][:, :, :, 0:D],
                                          v_in[:, :, :].rearrange("p i (h d) -> p i h d", h=H)).then_inc(s_vx, 1)

                if it.has(2):
                    pool.wait_ge(s_prep, (it.it + 2) * K_PREP + PREP_STAT)
                    inverse_root(mv, rstd, s_rstd, it.it + 2)
                if it.has(-2):
                    b, r = it.it - 2, it.par(-2)
                    pool.wait_ge(s_route, (b + 1) * K_ROUTE)
                    pool.wait_ge(s_zcp, b + 1)
                    hold(pool, s_held[2])
                    for c in range(2):
                        for i in range(NT):
                            nc.gpsimd.indirect_dma_start(
                                out=z_dram, out_offset=bass.IndirectOffsetOnAxis(ap=slot_u[:, c, i:i + 1], axis=0),
                                in_=z_row[c][:, i, :], in_offset=None).then_inc(s_sc, 16)
                if it.has(1):
                    split_weights(it.it + 1, it.kind + 1, 0)
                if it.has(-1):
                    pool.wait_ge(s_ln2, (it.it - 1) * K_LN2 + LN2_STAT)
                    inverse_root(mv2, rstd2, s_rstd2, it.it - 1)
                if it.has(1):
                    split_weights(it.it + 1, it.kind + 1, 1)
                    split_weights(it.it + 1, it.kind + 1, 2)
                if it.has(-1):
                    b, r = it.it - 1, it.par(-1)
                    pool.wait_ge(s_zh, b + 1)
                    pool.wait_ge(s_ln2, (b + 1) * K_LN2)
                    hold(pool, s_held[2])
                    nc.gpsimd.tensor_copy(z_row[1][:, :, 0:W], z_row[0][:, :, 0:W]).then_inc(s_zcp, 1)

            iterations(pool, body)
            pool.wait_ge(s_wst, 32 * 3 * E)
            pool.wait_ge(s_sc, 128 * B)

        @block.scalar
        def _(act):
            act.wait_ge(s_con, 64)

            def body(it):
                for s in range(H):
                    g, j = s // 4, s % 4
                    if it.has(0):
                        b, r = it.it, it.par()
                        q = b * 4 + g
                        for u in range(2):
                            n = b * 32 + 2 * s + u
                            act.wait_ge(s_b, n + 1)
                            if j == 0 and u == 0 and it.kind * 4 + g >= 2:
                                act.wait_ge(s_pv, q - 1)
                            nc.scalar.activation(probs[g % 2][:, j, 2 * u:2 * u + 2, :], exp_bank[u],
                                                 ACT.Exp, scale=0.25).then_inc(s_exp, 1)
                    if s == 1 and it.has(-2):
                        b = it.it - 2
                        act.wait_ge(s_route, b * K_ROUTE + ROUTE_D)
                        nc.scalar.activation(ediff[:, :], diff[:, :], ACT.Exp).then_inc(s_ed, 1)
                    if s == 5 and it.has(2):
                        b = it.it + 2
                        act.wait_ge(s_prep, b * K_PREP + PREP_QN)
                        if it.kind + 2 >= 1:
                            act.wait_ge(s_mw, it.use(1, "turn_q", 1) + 1)
                        nc.scalar.copy(q16[0][:, :, :], x_in[:, :, :]).then_inc(s_qh, 1)
                    if s == 3 and it.has(2):
                        b = it.it + 2
                        act.wait_ge(s_kin, (b + 1) * 16)
                        if it.kind + 2 >= 1:
                            act.wait_ge(s_kd, b * 96)
                        nc.scalar.copy(k16[0][:, :, :], kt_in[:, :, :]).then_inc(s_kh, 1)
                    if s == 11 and it.has(-1):
                        b, r = it.it - 1, it.par(-1)
                        act.wait_ge(s_ln2, b * K_LN2 + LN2_Z)
                        if it.kind - 1 >= 1:
                            act.wait_ge(s_sc, b * 128)
                        nc.scalar.copy(z_row[0][:, :, 0:W // 2].bitcast(F16), x2[:, :, :]).then_inc(s_zh, 1)
                    for m, name, i, lag in it.misc(s):
                        b, r = it.it + lag, it.par(lag)
                        if name == "max":
                            act.wait_ge(s_mw, m + 1)
                            if (it.kind + lag) * 4 + i >= 2:
                                act.wait_ge(s_mrow[(i + 2) % 4], (b if i < 2 else b + 1) * 64)
                            nc.scalar.copy(max_row[i % 2][:, :], misc16[0:4, 0:T]).then_inc(s_mr, 1)
                        if name == "turn":
                            act.wait_ge(s_mw, m + 1)
                            nc.scalar.copy(o_t[:, i, :], misc_bank).then_inc(s_mr, 1)
                        if name == "turn_q":
                            act.wait_ge(s_mw, m + 1)
                            if it.kind + lag >= 1:
                                act.wait_ge(s_qd, b * 96)
                            nc.scalar.copy(qt16[i][:, :, :].rearrange("p a t -> p (a t)"), misc16).then_inc(s_mr, 1)
                        if name == "turn_z":
                            act.wait_ge(s_mw, m + 1)
                            nc.scalar.copy(o_t[:, i, :], misc_bank).then_inc(s_mr, 1)
                        if name == "logits":
                            act.wait_ge(s_mw, m + 1)
                            nc.scalar.copy(logit_t[:, :], misc_bank[0:E, :]).then_inc(s_mr, 1)
                    if j == 3 and (it.has(0) and g >= 1 or g == 0 and it.has(-1)):
                        q = it.it * 4 + g - 1
                        act.wait_ge(s_pv, q + 1)
                        if it.kind * 4 + g - 1 >= 2:
                            lag, i = ((-1, 1), (-1, 2), (-1, 3), (0, 0))[g]
                            act.wait_ge(s_mw, it.use(lag, "heads", i) + 1)
                        nc.scalar.copy(heads[(g - 1) % 2][:, :], pv_bank).then_inc(s_hd, 1)

            iterations(act, body)

        @block.vector
        def _(dve):
            dve.wait_ge(s_con, 64)
            nc.vector.memset(q_stack[0][:, :, :].bitcast(F32), 0.0).then_inc(s_cst, 1)
            nc.vector.memset(q_stack[1][:, :, :].bitcast(F32), 0.0).then_inc(s_cst, 1)
            nc.vector.memset(fill[:, :, :], 0.0).then_inc(s_cst, 1)
            dve.wait_ge(s_cst, 3)
            nc.vector.tensor_copy(fill[:, :, W].bitcast(U32), con[:, C_TRASH:C_TRASH + SUB]).then_inc(s_cst, 1)
            dve.wait_ge(s_zero, 2)
            nc.vector.tensor_copy(ident16[:, :], ident).then_inc(s_cst, 1)
            nc.vector.tensor_copy(upper16[:, :], con[:, C_U:C_U + P]).then_inc(s_cst, 1)
            nc.vector.tensor_copy(run[:, :], con[:, C_REG:C_REG + E]).then_inc(s_cst, 1)
            nc.vector.tensor_copy(tok[:, :], con[:, C_TOK:C_TOK + NT]).then_inc(s_cst, 1)
            for r in range(2):
                for par in range(2):
                    row = 64 * par + STACK
                    nc.vector.tensor_scalar(k_stack[r][64 * par + 32:64 * par + 64, :, :],
                                            k_stack[r][64 * par + 32:64 * par + 64, :, :], 0.0,
                                            con[64 * par + 32:64 * par + 64, C_ROW:C_ROW + 1],
                                            ALU.mult, ALU.add).then_inc(s_cst, 1)
            dve.wait_ge(s_cst, 12)

            def take_max(it, s, i):
                if not it.has(1):
                    return
                n = (it.it + 1) * 64 + 4 * s + i
                dve.wait_ge(s_a, n + 1)
                nc.vector.tensor_reduce(mx[it.par(1)][:, i, s:s + 1], max_bank[i % 2], AX.X,
                                        ALU.max).then_inc(s_red, 1)

            def take_statistics(chain, src, st, agg):
                for i in range(NT):
                    chain.step(nc.vector.bn_stats(st[:, i, :], src[:, i, :]))
                chain.wait(dve)
                hold(dve, s_held[0])
                for i in range(NT):
                    chain.step(nc.vector.bn_aggr(agg[:, i, :], st[:, i, :]))

            def normalise(chain, src, agg, rs):
                for i in range(NT):
                    chain.step(nc.vector.tensor_scalar(src[:, i, :], src[:, i, :], agg[:, i, 0:1],
                                                       rs[:, i:i + 1], ALU.subtract, ALU.mult))

            def rank_experts(it):
                b = it.it - 2
                route.start(b)
                dve.wait_ge(s_mr, it.use(-2, "turn_l", 0) + 1)
                four = [P, NT, E, E]
                of_j = logit[:, :, :].unsqueeze(2).broadcast_to(four)
                of_e = logit[:, :, :].unsqueeze(3).broadcast_to(four)
                c1 = cmp1[:, :, :].rearrange("p i (e j) -> p i e j", e=E)
                c2 = cmp2[:, :, :].rearrange("p i (e j) -> p i e j", e=E)
                route.step(nc.vector.tensor_tensor(c1, of_j, of_e, ALU.is_gt))
                route.step(nc.vector.tensor_tensor(c2, of_j, of_e, ALU.is_equal))
                route.wait(dve)
                lower = con[:, C_LT:C_LT + E * E].unsqueeze(1).broadcast_to([P, NT, E * E])
                route.step(nc.vector.tensor_tensor(cmp2[:, :, :], cmp2[:, :, :], lower, ALU.mult))
                route.wait(dve)
                route.step(nc.vector.tensor_tensor(cmp1[:, :, :], cmp1[:, :, :], cmp2[:, :, :], ALU.add))
                route.wait(dve)
                route.step(nc.vector.tensor_reduce(rank[:, :], cmp1[:, :, :].rearrange("p i (e j) -> p (i e) j", e=E),
                                                   AX.X, ALU.add))
                route.wait(dve)
                for c in range(2):
                    route.step(nc.vector.tensor_scalar(hot[c][:, :], rank[:, :], float(c), None, ALU.is_equal))
                route.step(nc.vector.tensor_scalar(sel16[:, :], rank[:, :], 2.0, None, ALU.is_lt))
                assert route.n == ROUTE_SEL
                flat = logit[:, :, :].rearrange("p i e -> p (i e)")
                for c in range(2):
                    pick_one(c, flat, val[c][:, :])
                route.wait(dve)
                route.step(nc.vector.tensor_tensor(diff[:, :], val[1][:, :], val[0][:, :], ALU.subtract))
                assert route.n == ROUTE_D

            def pick_one(c, values, dst):
                route.wait(dve)
                route.step(nc.vector.tensor_tensor(pick[:, :], hot[c][:, :], values, ALU.mult))
                route.wait(dve)
                route.step(nc.vector.tensor_reduce(dst, pick[:, :].rearrange("p (i e) -> p i e", e=E), AX.X, ALU.add))

            def weigh_experts(it):
                b, r = it.it - 2, it.par(-2)
                dve.wait_ge(s_ed, b + 1)
                route.step(nc.vector.tensor_scalar(den[:, :], ediff[:, :], 1.0, None, ALU.add))
                route.wait(dve)
                route.step(nc.vector.reciprocal(gate[0][:, :], den[:, :]))
                route.wait(dve)
                route.step(nc.vector.tensor_tensor(gate[1][:, :], ediff[:, :], gate[0][:, :], ALU.mult))
                route.wait(dve)
                if it.kind - 2 >= 1:
                    dve.wait_ge(s_sc, b * 128)
                for c in range(2):
                    route.step(nc.vector.tensor_scalar(z_row[c][:, :, W + 1], gate[c][:, :], 1.0 / WSCALE,
                                                       None, ALU.mult))
                    route.step(nc.vector.tensor_copy(z_row[c][:, :, W].bitcast(U32), tok[:, :]))
                route.wait(dve)
                route.step(nc.vector.tensor_scalar(tok[:, :], tok[:, :], float(T), None, ALU.add))

            def find_slots(it, m):
                b, r = it.it - 2, it.par(-2)
                dve.wait_ge(s_mw, m + 1)
                route.step(nc.vector.tensor_tensor(
                    pos[:, :].rearrange("p (i e) -> p i e", e=E),
                    misc_bank[:, 0:NT * E].rearrange("p (i e) -> p i e", e=E),
                    run[:, :].unsqueeze(1).broadcast_to([P, NT, E]), ALU.add))
                route.wait(dve)
                nc.vector.tensor_tensor(run[:, :], run[:, :], misc_bank[:, NT * E:(NT + 1) * E],
                                        ALU.add).then_inc(s_mr, 1)
                dve.wait_ge(s_mr, m + 1)
                if it.kind - 2 >= 1:
                    dve.wait_ge(s_sc, b * 128)
                for c in range(2):
                    pick_one(c, pos[:, :], slot_f[:, c, :])
                route.wait(dve)
                route.step(nc.vector.tensor_copy(slot_u[:, :, :], slot_f[:, :, :]))
                assert route.n == K_ROUTE, route.n

            def body(it):
                for s in range(H):
                    g, j = s // 4, s % 4
                    for i in range(NT):
                        take_max(it, s, i)
                    if j == 3 and it.has(1):
                        b, r = it.it + 1, it.par(1)
                        dve.wait_ge(s_red, (b * 64) + 16 * (g + 1))
                        if (it.kind + 1) * 4 + g >= 1:
                            dve.wait_ge(s_mw, (it.use(0, "max", 3) if g == 0 else it.use(1, "max", g - 1)) + 1)
                        nc.vector.tensor_scalar(
                            neg_max[:, :, :].rearrange("p i (a b) -> p i a b", a=2),
                            mx[r][:, :, 4 * g:4 * g + 4].rearrange("p i (b a) -> p i a b", a=2),
                            -1.0, None, ALU.mult).then_inc(s_neg, 1)
                    if s == 3 and it.has(2):
                        b = it.it + 2
                        dve.wait_ge(s_xin, (b + 1) * 16)
                        if it.kind + 2 >= 1:
                            dve.wait_ge(s_qh, b)
                        prep.start(b)
                        take_statistics(prep, x_in, stats, mv)
                        assert prep.n == PREP_STAT
                    if s == 4 and it.has(2):
                        dve.wait_ge(s_rstd, (it.it + 3) * 2)
                        normalise(prep, x_in, mv, rstd)
                        assert prep.n == PREP_QN
                    if s == 6 and it.has(2):
                        b = it.it + 2
                        prep.wait(dve)
                        dve.wait_ge(s_qh, b + 1)
                        prep.step(nc.vector.tensor_tensor(q16[1][:, :, :], x_in[:, :, :], q16[0][:, :, :],
                                                          ALU.subtract))
                        dve.wait_ge(s_kh, b + 1)
                        prep.step(nc.vector.tensor_tensor(k16[1][:, :, :], kt_in[:, :, :], k16[0][:, :, :],
                                                          ALU.subtract))
                        assert prep.n == K_PREP
                    if s == 9 and it.has(-1):
                        b, r = it.it - 1, it.par(-1)
                        ln2.start(b)
                        take_statistics(ln2, x2, stats2, mv2)
                        assert ln2.n == LN2_STAT
                    if s == 10 and it.has(-1):
                        b = it.it - 1
                        dve.wait_ge(s_rstd2, (b + 1) * 2)
                        dve.wait_ge(s_x2st, (b + 1) * 16)
                        normalise(ln2, x2, mv2, rstd2)
                        assert ln2.n == LN2_Z
                    if s == 12 and it.has(-1):
                        b, r = it.it - 1, it.par(-1)
                        ln2.wait(dve)
                        dve.wait_ge(s_zh, b + 1)
                        ln2.step(nc.vector.tensor_tensor(z_row[0][:, :, W // 2:W].bitcast(F16), x2[:, :, :],
                                                         z_row[0][:, :, 0:W // 2].bitcast(F16),
                                                         ALU.subtract))
                        assert ln2.n == K_LN2
                    if s == 0 and it.has(-2):
                        rank_experts(it)
                    if s == 2 and it.has(-2):
                        weigh_experts(it)
                    for m, name, i, lag in it.misc(s):
                        b, r = it.it + lag, it.par(lag)
                        if name == "turn_l":
                            dve.wait_ge(s_mw, m + 1)
                            nc.vector.tensor_copy(logit[:, :, :].rearrange("p i e -> p (i e)"),
                                                  misc_bank[:, 0:NT * E]).then_inc(s_mr, 1)
                        if name == "prefix":
                            find_slots(it, m)
                        if name == "heads":
                            dve.wait_ge(s_mw, m + 1)
                            src = misc_bank.rearrange("p (i h c) -> p i h c", i=NT, h=4)
                            nc.vector.reciprocal(recip[:, :, :], src[:, :, :, D]).then_inc(s_rec, 1)
                            dve.wait_ge(s_rec, b * 4 + (i + 1))
                            nc.vector.tensor_tensor(
                                o_norm[:, :, 64 * i:64 * i + 64].rearrange("p i (h d) -> p i h d", h=4),
                                src[:, :, :, 0:D], recip[:, :, :].unsqueeze(3).broadcast_to([P, NT, 4, D]),
                                ALU.mult).then_inc(s_mr, 1)
                        if name == "project":
                            dve.wait_ge(s_mw, m + 1)
                            dve.wait_ge(s_xres, b + 1)
                            if it.kind + lag >= 1:
                                dve.wait_ge(s_x2st, b * 16)
                            nc.vector.tensor_tensor(x2[:, 2 * i:2 * i + 2, :],
                                                    misc_bank.rearrange("p (i c) -> p i c", i=2),
                                                    x_res[:, 2 * i:2 * i + 2, :], ALU.add).then_inc(s_mr, 1)
                            if i == 1:
                                dve.wait_ge(s_mr, m + 1)

            iterations(dve, body)

        @block.tensor
        def _(pe):
            pe.wait_ge(s_cst, 12)
            pe.wait_ge(s_con, 64)
            pe.wait_ge(s_zero, 8)

            def scores_ts(it, s, i):
                if not it.has(1):
                    return
                b, r = it.it + 1, it.par(1)
                n = b * 64 + 4 * s + i
                if i == 0 and s % 4 == 0:
                    pe.wait_ge(s_stk[s // 4], (b + 1) * 64)
                if it.kind + 1 >= 1 or 4 * s + i >= 2:
                    pe.wait_ge(s_red, n - 1)
                nc.tensor.matmul(max_bank[i % 2], q_stack[r][:, s, i * P:(i + 1) * P],
                                 k_stack[r][:, s // 2, :], start=True, stop=True).then_inc(s_a, 1)

            def scores_st(it, s, u):
                if not it.has(0):
                    return
                b, r = it.it, it.par()
                n = b * 32 + 2 * s + u
                if s % 4 == 0 and u == 0:
                    pe.wait_ge(s_mrow[s // 4], (b + 1) * 64)
                if it.kind >= 1 or 2 * s + u >= 2:
                    pe.wait_ge(s_exp, n - 1)
                for v in range(2):
                    k = 2 * u + v
                    mm = nc.tensor.matmul(exp_bank[u][:, v, :], k_stack[r][:, s // 2, k * P:(k + 1) * P],
                                          q_stack[r][:, s, :], start=True, stop=True)
                mm.then_inc(s_b, 1)

            def weigh(it, g, j):
                if not (it.has(0) and g >= 1 or g == 0 and it.has(-1)):
                    return
                q = it.it * 4 + g - 1
                gq, r = (g - 1) % 4, it.par() if g else it.par(-1)
                if j == 0:
                    pe.wait_ge(s_exp, q * 8 + 8)
                    if it.kind * 4 + g - 1 >= 1:
                        pe.wait_ge(s_hd, q)
                    if gq == 0:
                        pe.wait_ge(s_vx, it.it + 1)
                for n in range(4):
                    mm = nc.tensor.matmul(pv_bank[32 * n:32 * n + 32, :], v_ext[r][:, j, 4 * gq + n, :],
                                          probs[gq % 2][:, n, j, :], start=(j == 0), stop=(j == NT - 1),
                                          tile_position=(0, 32 * n))
                if j == NT - 1:
                    mm.then_inc(s_pv, 1)

            def misc(it, s):
                for m, name, i, lag in it.misc(s):
                    b = it.it + lag
                    ge(pe, s_mr, m)
                    if name == "turn_l":
                        hold(pe, s_held[1])
                    if name == "max":
                        pe.wait_ge(s_neg, b * 4 + (i + 1))
                        for t in range(NT):
                            mm = nc.tensor.transpose(misc16[0:4, t * P:(t + 1) * P], neg_max[:, t, :], ident16[:, :])
                    if name == "heads":
                        pe.wait_ge(s_hd, b * 4 + (i + 1))
                        for t in range(NT):
                            mm = nc.tensor.transpose(misc_bank[:, t * P:(t + 1) * P],
                                                     heads[i % 2][:, t * P:(t + 1) * P], ident)
                    if name == "turn":
                        for t in range(NT):
                            mm = nc.tensor.transpose(misc_bank[:, t * P:(t + 1) * P],
                                                     o_norm[:, t, i * P:(i + 1) * P], ident)
                    if name == "project":
                        for t in range(2):
                            for k in range(2):
                                tt = 2 * i + t
                                mm = nc.tensor.matmul(misc_bank[:, t * W:(t + 1) * W],
                                                      o_t[:, k, tt * P:(tt + 1) * P], wp_sb[:, k, :],
                                                      start=(k == 0), stop=(k == 1))
                    if name == "turn_q":
                        pe.wait_ge(s_qh, b + 1)
                        pe.wait_ge(s_prep, b * K_PREP + PREP_QL)
                        for a in range(2):
                            for t in range(NT):
                                mm = nc.tensor.transpose(misc16[:, a * T + t * P:a * T + (t + 1) * P],
                                                         q16[i][:, t, a * P:(a + 1) * P], ident16[:, :])
                    if name == "turn_z":
                        pe.wait_ge(s_ln2, b * K_LN2 + LN2_Z)
                        for t in range(NT):
                            mm = nc.tensor.transpose(misc_bank[:, t * P:(t + 1) * P],
                                                     x2[:, t, i * P:(i + 1) * P], ident)
                    if name == "logits":
                        for k in range(2):
                            mm = nc.tensor.matmul(misc_bank[0:E, :], wg_sb[:, k, :], o_t[:, k, :],
                                                  start=(k == 0), stop=(k == 1))
                    if name == "turn_l":
                        for t in range(NT):
                            mm = nc.tensor.transpose(misc_bank[:, t * E:(t + 1) * E],
                                                     logit_t[:, t * P:(t + 1) * P], ident[0:E, 0:E])
                    if name == "prefix":
                        pe.wait_ge(s_route, b * K_ROUTE + ROUTE_SEL)
                        nc.tensor.matmul(misc_bank[:, 0:NT * E], upper16[:, :], sel16[:, :], start=True,
                                         stop=False, skip_group_check=True)
                        for t in range(1, NT + 1):
                            for t0 in range(t):
                                mm = nc.tensor.matmul(misc_bank[:, t * E:(t + 1) * E], ones16[:, :],
                                                      sel16[:, t0 * E:(t0 + 1) * E], start=False,
                                                      stop=(t == NT and t0 == t - 1), skip_group_check=True)
                    mm.then_inc(s_mw, 1)

            def body(it):
                for s in range(H):
                    g, j = s // 4, s % 4
                    scores_st(it, s, 0)
                    scores_ts(it, s, 0)
                    scores_ts(it, s, 1)
                    scores_st(it, s, 1)
                    scores_ts(it, s, 2)
                    scores_ts(it, s, 3)
                    weigh(it, g, j)
                    misc(it, s)

            iterations(pe, body)

        attention.close()
        att.close()

        with ExitStack() as ffn:
            def sf(name, shape, dt=F32):
                return ffn.enter_context(nc.sbuf_tensor(name, shape, dt))

            cnt = sf("cnt", [P, E])
            cmp3 = sf("cmp3", [P, E, NCNT])
            n_tiles = sf("n_tiles", [P, E])
            cmp4 = sf("cmp4", [P, E, E])
            t_end = sf("t_end", [P, E])
            t_begin = sf("t_begin", [P, E])
            origin = sf("origin", [P, E])
            cmp5 = sf("cmp5", [P, FFN_TILES, E])
            cmp6 = sf("cmp6", [P, FFN_TILES, E])
            expert = sf("expert", [P, FFN_TILES])
            row_f = sf("row_f", [P, FFN_TILES])
            row_tab = sf("row_tab", [P, FFN_TILES], I32)
            exp_tab = sf("exp_tab", [P, FFN_TILES], I32)
            pad_tab = sf("pad_tab", [P, E], I32)
            z_in = [sf(f"z_in{i}", [P, SUB, ROW]) for i in range(2)]
            aim = [sf(f"aim{i}", [P, SUB, 2]) for i in range(2)]
            w12 = [sf(f"w12_{i}", [P, 2, 2, 2, HC * HP], F16) for i in range(2)]
            w3 = [sf(f"w3_{i}", [HP, 2, HC, W], F16) for i in range(2)]
            zt16 = [sf(f"zt16_{i}", [P, 2, 2, SLOTS], F16) for i in range(2)]
            silu = [sf(f"silu{i}", [HP, SLOTS]) for i in range(2)]
            hid = [sf(f"hid{i}", [HP, SLOTS]) for i in range(2)]
            hid16 = sf("hid16", [HP, HC, 2, SLOTS], F16)
            y = [sf(f"y{i}", [P, SUB, W]) for i in range(2)]
            y_bank = [ps[:, 4, 0:W], ps[:, 5, 0:W]]
            turn16 = ps[:, 6, :].bitcast(F16)

            f_pad = sem("f_pad")
            f_z = [sem("f_z0"), sem("f_z1")]
            f_w = [sem("f_w0"), sem("f_w1")]
            f_aim = sem("f_aim")
            f_turn = sem("f_turn")
            f_zt = sem("f_zt")
            f_up = sem("f_up")
            f_silu = sem("f_silu")
            f_hid = sem("f_hid")
            f_hi, f_lo = sem("f_hi"), sem("f_lo")
            f_down = sem("f_down")
            f_y = sem("f_y")
            f_add = sem("f_add")
            K_TAB = 16

            block2 = ffn.enter_context(nc.Block())

            @block2.vector
            def _(dve):
                n = 0

                def step(ins):
                    nonlocal n
                    n += 1
                    ins.then_inc(s_tab, 1)
                    dve.wait_ge(s_tab, n)

                reg = con[:, C_REG:C_REG + E]
                tt = nc.vector.tensor_tensor
                step(tt(cnt[:, :], run[:, :], reg, ALU.subtract))
                step(tt(cmp3[:, :, :], cnt[:, :].unsqueeze(2).broadcast_to([P, E, NCNT]),
                        con[:, C_CNT:C_CNT + NCNT].unsqueeze(1).broadcast_to([P, E, NCNT]), ALU.is_gt))
                step(nc.vector.tensor_reduce(n_tiles[:, :], cmp3[:, :, :], AX.X, ALU.add))
                step(tt(cmp4[:, :, :], con[:, C_LE:C_LE + E * E].rearrange("p (e j) -> p e j", e=E),
                        n_tiles[:, :].unsqueeze(1).broadcast_to([P, E, E]), ALU.mult))
                step(nc.vector.tensor_reduce(t_end[:, :], cmp4[:, :, :], AX.X, ALU.add))
                step(tt(t_begin[:, :], t_end[:, :], n_tiles[:, :], ALU.subtract))
                step(nc.vector.scalar_tensor_tensor(out=origin[:, :], in0=t_begin[:, :], scalar=-float(SLOTS),
                                                    in1=reg, op0=ALU.mult, op1=ALU.add))
                big = [P, FFN_TILES, E]
                step(tt(cmp5[:, :, :], t_end[:, :].unsqueeze(1).broadcast_to(big),
                        con[:, C_K:C_K + FFN_TILES].unsqueeze(2).broadcast_to(big), ALU.is_le))
                step(nc.vector.tensor_reduce(expert[:, :], cmp5[:, :, :], AX.X, ALU.add))
                step(tt(cmp5[:, :, :], expert[:, :].unsqueeze(2).broadcast_to(big),
                        con[:, C_E:C_E + E].unsqueeze(1).broadcast_to(big), ALU.is_equal))
                step(tt(cmp6[:, :, :], origin[:, :].unsqueeze(1).broadcast_to(big),
                        con[:, C_KS:C_KS + FFN_TILES].unsqueeze(2).broadcast_to(big), ALU.add))
                step(tt(cmp5[:, :, :], cmp5[:, :, :], cmp6[:, :, :], ALU.mult))
                step(nc.vector.tensor_reduce(row_f[:, :], cmp5[:, :, :], AX.X, ALU.add))
                step(nc.vector.tensor_scalar(row_tab[:, :], row_f[:, :], float(E * REGION), None, ALU.add))
                step(nc.vector.tensor_scalar(exp_tab[:, :], expert[:, :], float(E - 1), None, ALU.min))
                step(nc.vector.tensor_copy(pad_tab[:, :], run[:, :]))
                assert n == K_TAB

                def body(k, half, par, least):
                    if least >= 2:
                        dve.wait_ge(f_add, (k - 1) * 32)
                    dve.wait_ge(f_z[par], half * 16 + 16)
                    nc.vector.tensor_copy(aim[par][:, :, :].bitcast(I32),
                                          z_in[par][:, :, W:W + 2].bitcast(I32)).then_inc(f_aim, 1)
                    for m in range(HC + 1):
                        if m < HC:
                            u, bank = k * HC + m, (m + 2 * par) % 4
                            dve.wait_ge(f_silu, u + 1)
                            if least * HC + m >= 2:
                                dve.wait_ge(f_hi, u - 1)
                                dve.wait_ge(f_lo, u - 1)
                            nc.vector.scalar_tensor_tensor(
                                out=hid[m % 2][:, :], in0=ps[0:HP, bank, W:2 * W], scalar=1.0 / WSCALE,
                                in1=silu[m % 2][:, :], op0=ALU.mult, op1=ALU.mult).then_inc(f_hid, 1)
                        if m >= 1:
                            u = k * HC + (m - 1)
                            dve.wait_ge(f_hi, u + 1)
                            nc.vector.tensor_tensor(hid16[:, m - 1, 1, :], hid[(m - 1) % 2][:, :],
                                                    hid16[:, m - 1, 0, :], ALU.subtract).then_inc(f_lo, 1)
                    dve.wait_ge(f_aim, k + 1)
                    for t in range(SUB):
                        dve.wait_ge(f_down, k * SUB + (t + 1))
                        nc.vector.tensor_scalar(y[par][:, t, :], y_bank[t], aim[par][:, t, 1:2], None,
                                                ALU.mult).then_inc(f_y, 1)

                ffn_tiles(dve, body)

            @block2.scalar
            def _(act):
                def keep_turned(k, par, least):
                    act.wait_ge(f_turn, k + 1)
                    nc.scalar.copy(zt16[par][:, :, :, :].rearrange("p k a s -> p (k a s)"),
                                   turn16).then_inc(f_zt, 1)

                keep_turned(0, 0, 0)

                def body(k, half, par, least):
                    for m in range(HC + 1):
                        if m < HC:
                            u, bank = k * HC + m, (m + 2 * par) % 4
                            act.wait_ge(f_up, u + 1)
                            if least * HC + m >= 2:
                                act.wait_ge(f_hid, u - 1)
                            nc.scalar.activation(silu[m % 2][:, :], ps[0:HP, bank, 0:W], ACT.Silu,
                                                 scale=1.0 / WSCALE).then_inc(f_silu, 1)
                        if m >= 1:
                            u = k * HC + (m - 1)
                            act.wait_ge(f_hid, u + 1)
                            if least >= 1:
                                act.wait_ge(f_down, k * SUB)
                            nc.scalar.copy(hid16[:, m - 1, 0, :], hid[(m - 1) % 2][:, :]).then_inc(f_hi, 1)
                    if least < FFN_TILES - 1:
                        keep_turned(k + 1, 1 - par, least + 1)

                ffn_tiles(act, body)

            @block2.tensor
            def _(pe):
                def turn(k, half, par, least):
                    pe.wait_ge(f_z[par], half * 16 + 16)
                    if least >= 1:
                        pe.wait_ge(f_zt, k)
                    rows = z_in[par][:, :, 0:W].bitcast(F16).rearrange("p s (a k c) -> p s a k c", a=2, k=2)
                    for kk in range(2):
                        for a in range(2):
                            for t in range(SUB):
                                col = (kk * 2 + a) * SLOTS + t * P
                                mm = nc.tensor.transpose(turn16[:, col:col + P], rows[:, t, a, kk, :], ident16[:, :])
                    mm.then_inc(f_turn, 1)

                turn(0, 0, 0, 0)

                def body(k, half, par, least):
                    pe.wait_ge(f_zt, k + 1)
                    pe.wait_ge(f_w[par], half * 32 + 32)
                    z16, w = zt16[par], w12[par]
                    for m in range(HC):
                        u, bank = k * HC + m, (m + 2 * par) % 4
                        if least * HC + m >= 4:
                            pe.wait_ge(f_hid, u - 3)
                        cols = slice(m * HP, (m + 1) * HP)
                        for c in range(2):
                            dst = ps[0:HP, bank, c * W:(c + 1) * W]
                            for kk in range(2):
                                lo = nc.tensor.matmul(dst, w[:, c, 1, kk, cols], z16[:, kk, 0, :],
                                                      start=(kk == 0), stop=False)
                                nc.tensor.matmul(dst, w[:, c, 0, kk, cols], z16[:, kk, 1, :],
                                                 start=False, stop=False)
                                mm = nc.tensor.matmul(dst, w[:, c, 0, kk, cols], z16[:, kk, 0, :],
                                                      start=False, stop=(kk == 1))
                        mm.then_inc(f_up, 1)
                    if least < FFN_TILES - 1:
                        turn(k + 1, half + par, 1 - par, least + 1)
                    if least >= 1:
                        pe.wait_ge(f_y, k * SUB)
                    for m in range(HC):
                        pe.wait_ge(f_lo, k * HC + (m + 1))
                        for t in range(SUB):
                            h = [hid16[:, m, a, t * P:(t + 1) * P] for a in range(2)]
                            nc.tensor.matmul(y_bank[t], h[1], w3[par][:, 0, m, :], start=(m == 0), stop=False)
                            nc.tensor.matmul(y_bank[t], h[0], w3[par][:, 1, m, :], start=False, stop=False)
                            mm = nc.tensor.matmul(y_bank[t], h[0], w3[par][:, 0, m, :], start=False,
                                                  stop=(m == HC - 1))
                            if m == HC - 1:
                                mm.then_inc(f_down, 1)

                ffn_tiles(pe, body)

            @block2.sync
            def _(sp):
                sp.wait_ge(s_tab, K_TAB)
                for e in range(E):
                    first = sp.value_load(pad_tab[0:1, e:e + 1], min_val=0, max_val=E * REGION)
                    sp.dma_start(z_dram[bass.ds(first, SLOTS), :].rearrange("(s p) c -> p s c", p=P),
                                 fill[:, :, :]).then_inc(f_pad, 16)
                sp.wait_ge(f_pad, 16 * E)

                def body(k, half, par, least):
                    first = sp.value_load(row_tab[0:1, at(k)], min_val=0, max_val=E * REGION)
                    e = sp.value_load(exp_tab[0:1, at(k)], min_val=0, max_val=E - 1)
                    if least >= 2:
                        sp.wait_ge(f_turn, k - 1)
                        sp.wait_ge(f_aim, k - 1)
                    hold(sp, s_held[3])
                    sp.dma_start(z_in[par][:, :, :], z_dram[bass.ds(first, SLOTS), :].rearrange(
                        "(s p) c -> p s c", p=P)).then_inc(f_z[par], 16)
                    if least >= 2:
                        sp.wait_ge(f_down, (k - 1) * SUB)
                    hold(sp, s_held[3])
                    sp.dma_start(w12[par][:, :, :, :, :].rearrange("p c a k h -> p (c a k h)"),
                                 w12_dram[bass.ds(e, 1)].rearrange("o p c a h -> p (o c a h)")
                                 ).then_inc(f_w[par], 16)
                    sp.dma_start(w3[par][:, :, :, :].rearrange("p a m c -> p (a m c)"),
                                 w3_dram[bass.ds(e, 1)].rearrange("o p a h -> p (o a h)")
                                 ).then_inc(f_w[par], 16)

                ffn_tiles(sp, body)

            @block2.gpsimd
            def _(pool):
                def body(k, half, par, least):
                    for t in range(SUB):
                        pool.wait_ge(f_y, k * SUB + (t + 1))
                        if least or t:
                            pool.wait_ge(f_add, (k * SUB + t) * 16)
                        hold(pool, s_held[2])
                        nc.gpsimd.indirect_dma_start(
                            out=out, out_offset=bass.IndirectOffsetOnAxis(ap=aim[par][:, t, 0:1].bitcast(U32), axis=0),
                            in_=y[par][:, t, :], in_offset=None, compute_op=ALU.add).then_inc(f_add, 16)

                ffn_tiles(pool, body)
                pool.wait_ge(f_add, 16 * SUB * FFN_TILES)


def kernel(x, ctx_1024, L0_xattn_w_proj, L0_xattn_b_proj, L0_ffn_Wg, L0_ffn_W1, L0_ffn_W2, L0_ffn_W3):
    import numpy as np
    import concourse.bacc as bacc
    from concourse.bass_utils import run_bass_kernel_spmd

    def tiles(a):
        return np.ascontiguousarray(np.asarray(a).reshape(B, NT, P, W).transpose(0, 2, 1, 3))

    def padded(a, axis):
        widths = [(0, 0)] * a.ndim
        widths[axis] = (0, HC * HP - HID)
        return np.pad(a, widths)

    c = np.asarray(ctx_1024)
    x_q = np.asarray(x).reshape(B, T, PAIRS, 2, D).transpose(0, 1, 3, 2, 4)
    k_t = c.reshape(B, T, PAIRS, 2, D).transpose(0, 2, 4, 3, 1).reshape(B, P, 2, T)
    w12 = np.stack([padded(np.asarray(w), 1).reshape(E, HC * HP, 2, P).transpose(0, 3, 2, 1)
                    for w in (L0_ffn_W1, L0_ffn_W2)], axis=1).reshape(E, 2, P, 2 * HC * HP)
    w3 = padded(np.asarray(L0_ffn_W3), 2).reshape(E, W, HC, HP).transpose(0, 3, 2, 1).reshape(E, HP, HC * W)
    wp = np.asarray(L0_xattn_w_proj).T.reshape(2, P, W).transpose(1, 0, 2)
    wg = np.asarray(L0_ffn_Wg).T.reshape(2, P, E).transpose(1, 0, 2)
    arrays = {"x": tiles(x), "x_q": tiles(x_q), "v": tiles(c), "k_t": k_t, "w_proj": wp, "b_proj": np.asarray(L0_xattn_b_proj),
              "w_gate": wg, "w12": w12, "w3": w3, "const": constants()}
    arrays = {k: np.ascontiguousarray(v) for k, v in arrays.items()}
    nc = bacc.Bacc("TRN2", target_bir_lowering=False, num_devices=1)
    d = {k: nc.dram_tensor(f"in_{k}", v.shape, F32, kind="ExternalInput").ap() for k, v in arrays.items()}
    out = nc.dram_tensor("out", (TOKENS + SLOTS, W), F32, kind="ExternalOutput").ap()
    build(nc, d["x_q"], d["x"], d["v"], d["k_t"], d["w_proj"], d["b_proj"], d["w_gate"], d["w12"], d["w3"],
          d["const"], out)
    r = run_bass_kernel_spmd(nc, [{f"in_{k}": v for k, v in arrays.items()}], core_ids=[0])
    return r.results[0]["out"][:TOKENS].reshape(B, T, W)
```

```python
from contextlib import ExitStack

import concourse.bass as bass
from concourse import mybir

ALU = mybir.AluOpType
ACT = mybir.ActivationFunctionType
AX = mybir.AxisListType
F32 = mybir.dt.float32
F16 = mybir.dt.float16
I32 = mybir.dt.int32
U32 = mybir.dt.uint32

P = 128
B, T, W = 8, 512, 256
H, D = 16, 16
NT = T // P
PAIRS = H // 2
STACK = 3 * D
QROWS = STACK + 1
E, HID = 8, 682
FULL = HID // P
HC = FULL + 1
HALF = P // 2
UP = (2 * FULL + 1) * P
TOKENS = B * T
SLOTS = 256
SUB = SLOTS // P
FIRM_TILES = 2 * TOKENS // SLOTS
FFN_TILES = FIRM_TILES + E - 1
REGION = TOKENS + SLOTS
ROW = W + 2
WSCALE = 256.0
EPS = 1e-5

C_ID = 0
C_U = C_ID + P
C_LT = C_U + P
C_LE = C_LT + E * E
C_TRASH = C_LE + E * E
C_TOK = C_TRASH + SUB
C_REG = C_TOK + NT
C_CNT = C_REG + E
NCNT = TOKENS // SLOTS
C_K = C_CNT + NCNT
C_KS = C_K + FFN_TILES
C_E = C_KS + FFN_TILES
C_ROW = C_E + E
C_EPS = C_ROW + 1
C_POW = C_EPS + 1
C_ONE = C_POW + 1
NCONST = C_ONE + 1


def constants():
    import numpy as np

    c = np.zeros((P, NCONST), np.float32)
    p = np.arange(P)
    c[:, C_ID:C_ID + P] = np.eye(P)
    c[:, C_U:C_U + P] = p[:, None] < p[None, :]
    e = np.arange(E)
    c[:, C_LT:C_LT + E * E] = (e[None, :] < e[:, None]).reshape(-1)
    c[:, C_LE:C_LE + E * E] = (e[None, :] <= e[:, None]).reshape(-1)
    c[:, C_TRASH:C_TRASH + SUB] = TOKENS + p[:, None] + P * np.arange(SUB)
    c[:, C_TOK:C_TOK + NT] = p[:, None] + P * np.arange(NT)
    c[:, C_REG:C_REG + E] = REGION * e
    c[:, C_CNT:C_CNT + NCNT] = SLOTS * np.arange(NCNT)
    c[:, C_K:C_K + FFN_TILES] = np.arange(FFN_TILES)
    c[:, C_KS:C_KS + FFN_TILES] = SLOTS * np.arange(FFN_TILES) - E * REGION
    c[:, C_E:C_E + E] = e
    c[:, C_ROW] = p % 64 == STACK
    c[:, C_EPS] = EPS
    c[:, C_POW] = -0.5
    c[:, C_ONE] = 1.0
    return c


MISC = [
    (1, "max", 3, 0), (2, "heads", 2, -1), (4, "prefix", 0, -2), (8, "max", 0, 1),
    (9, "heads", 3, -1), (12, "turn", 0, -1), (13, "turn", 1, -1), (14, "project", 0, -1),
    (15, "project", 1, -1), (16, "max", 1, 1), (17, "heads", 0, 0), (18, "turn_q", 0, 2),
    (21, "turn_q", 1, 2), (23, "turn_z", 0, -1), (24, "turn_z", 1, -1), (25, "max", 2, 1),
    (26, "heads", 1, 0), (29, "logits", 0, -1), (31, "turn_l", 0, -1),
]
FIRST, LAST = -2, B + 1
LOOP = (2, B - 2)


def active(lag, it):
    return 0 <= it + lag < B


def misc_before(it):
    return sum(active(lag, i) for i in range(FIRST, it) for _, _, _, lag in MISC)


class Iteration:

    def __init__(self, it, kind):
        self.it, self.kind = it, kind

    def has(self, lag):
        return active(lag, self.kind)

    def par(self, lag=0):
        return (self.kind + lag) % 2

    def misc(self, half_slot):
        before = misc_before(self.kind)
        if not isinstance(self.it, int):
            before = misc_before(LOOP[0]) + len(MISC) * (self.it - LOOP[0])
        n, out = 0, []
        for s, name, i, lag in MISC:
            if active(lag, self.kind):
                if s == half_slot:
                    out.append((before + n, name, i, lag))
                n += 1
        return out

    def use(self, lag, name, i):
        n = [k for k, e in enumerate(MISC) if e[1] == name and e[2] == i and e[3] in (lag, lag + 1)][0]
        delta = lag - MISC[n][3]
        if isinstance(self.it, int):
            k = self.kind + delta
            return misc_before(k) + sum(active(e[3], k) for e in MISC[:n])
        assert delta == 0 or n > 2
        return misc_before(LOOP[0]) + len(MISC) * (self.it - LOOP[0] + delta) + n


def hold(eng, passed):
    eng.sem_inc(passed, 1)


def at(b):
    return slice(b, b + 1) if isinstance(b, int) else bass.ds(b, 1)


def iterations(eng, body, prepare=None):
    body(Iteration(FIRST, FIRST))
    if prepare:
        prepare()
    for it in range(FIRST + 1, LOOP[0]):
        body(Iteration(it, it))
    with eng.Fori(0, (LOOP[1] - LOOP[0]) // 2) as i:
        for par in range(2):
            body(Iteration(i * 2 + (LOOP[0] + par), LOOP[0] + par))
    for it in range(LOOP[1], LAST + 1):
        body(Iteration(it, it))


def ffn_tiles(eng, total, *steps):
    for k in range(2):
        for step, _ in steps:
            step(k, 0, k, k)
    with eng.Fori(0, FIRM_TILES // 2 - 1) as i:
        for par in range(2):
            for step, _ in steps:
                step(i * 2 + (2 + par), i + 1, par, 2 + par)
    with eng.Fori(0, (FFN_TILES - FIRM_TILES) // 2) as i:
        for par in range(2):
            for step, ahead in steps:
                with eng.If(total > i * 2 + (FIRM_TILES + par - ahead)):
                    step(i * 2 + (FIRM_TILES + par), i + FIRM_TILES // 2, par, FIRM_TILES + par)
    last = FFN_TILES - 1
    for step, ahead in steps:
        with eng.If(total > last - ahead):
            step(last, last // 2, last % 2, last)


def ge(eng, sem, value):
    if not isinstance(value, int) or value > 0:
        eng.wait_ge(sem, value)


def bank_of(i):
    return 1 if i == 63 else i % 3


def uses_back(i):
    return {0: 4, 1: 2, 2: 4, 63: 2}.get(i, 3)


class Chain:

    def __init__(self, sem, per):
        self.sem, self.per = sem, per

    def start(self, b):
        self.b, self.n = b, 0

    def step(self, ins):
        self.n += 1
        ins.then_inc(self.sem, 1)

    def wait(self, eng):
        eng.wait_ge(self.sem, self.b * self.per + self.n)


PREP_STAT, PREP_QN = NT * 2, NT * 3
K_PREP = PREP_QN
LN2_STAT, LN2_Z = NT * 2, NT * 3
K_LN2 = LN2_Z
K_ROUTE = 27
ROUTE_SEL, ROUTE_D = 8, 13


def build(nc, xq_l, x_l, v_l, kT_l, wp_l, bias, wg_l, w12_l, w3_l, const, out):
    ctx = ExitStack()
    with ctx:
        def sb(name, shape, dt=F32):
            return ctx.enter_context(nc.sbuf_tensor(name, shape, dt))

        def sem(name):
            return ctx.enter_context(nc.semaphore(name))

        q_dram = nc.dram_tensor("q_parts", (2, 2, PAIRS, QROWS, T), F16, kind="Internal").ap()
        k_dram = nc.dram_tensor("k_parts", (2, 2, PAIRS, STACK, T), F16, kind="Internal").ap()
        z_dram = nc.dram_tensor("slots", ((E + 1) * REGION, ROW), F32, kind="Internal").ap()
        w12_dram = nc.dram_tensor("w12_parts", (E, P, 2, 2, UP), F16, kind="Internal").ap()
        w3_dram = nc.dram_tensor("w3_parts", (E, P, 2, HC * W), F16, kind="Internal").ap()

        con = sb("con", [P, NCONST])
        ident = con[:, C_ID:C_ID + P]
        slot_u = sb("slot_u", [P, 2, NT], U32)
        z_row = [sb(f"z_row{i}", [P, NT, ROW]) for i in range(2)]
        ident16 = sb("ident16", [P, P], F16)
        upper16 = sb("upper16", [P, P], F16)
        ones16 = sb("ones16", [P, P], F16)
        scale_w = sb("scale_w", [P, 1])
        bias_sb = sb("bias_sb", [P, W])
        wp_sb = sb("wp_sb", [P, 2, W])
        wg_sb = sb("wg_sb", [P, 2, E])
        fill = sb("fill", [P, SUB, ROW])
        run = sb("run", [P, E])

        att = ExitStack()

        def sa(name, shape, dt=F32):
            return att.enter_context(nc.sbuf_tensor(name, shape, dt))

        x_in = sa("x_in", [P, NT, W])
        kt_in = sa("kt_in", [P, 2, T])
        v_in = sa("v_in", [P, NT, W])
        q_stack = [sa(f"q_stack{i}", [P, H, T], F16) for i in range(2)]
        k_stack = [sa(f"k_stack{i}", [P, PAIRS, T], F16) for i in range(2)]
        v_ext = [sa(f"v_ext{i}", [P, NT, H, 32]) for i in range(2)]
        probs = [sa(f"probs{i}", [P, 4, NT, T]) for i in range(2)]
        heads = [sa(f"heads{i}", [P, T]) for i in range(2)]
        stats = sa("stats", [P, NT, 6])
        mv = sa("mv", [P, NT, 2])
        rstd = sa("rstd", [P, NT])
        q16 = [sa(f"q16_{i}", [P, NT, W], F16) for i in range(2)]
        qt16 = [sa(f"qt16_{i}", [P, 2, T], F16) for i in range(2)]
        k16 = [sa(f"k16_{i}", [P, 2, T], F16) for i in range(2)]
        mx = [sa(f"mx{i}", [P, NT, H]) for i in range(2)]
        neg_max = sa("neg_max", [P, NT, 4], F16)
        max_row = [sa(f"max_row{i}", [4, T], F16) for i in range(2)]
        recip = sa("recip", [P, NT, 4])
        o_norm = sa("o_norm", [P, NT, W])
        o_t = sa("o_t", [P, 2, T])
        x_res = sa("x_res", [P, NT, W])
        x2 = sa("x2", [P, NT, W])
        stats2 = sa("stats2", [P, NT, 6])
        mv2 = sa("mv2", [P, NT, 2])
        rstd2 = sa("rstd2", [P, NT])
        logit_t = sa("logit_t", [E, T])
        logit = sa("logit", [P, NT, E])
        cmp1 = sa("cmp1", [P, NT, E * E], F16)
        cmp2 = sa("cmp2", [P, NT, E * E], F16)
        rank = sa("rank", [P, NT * E])
        hot = [sa(f"hot{i}", [P, NT * E]) for i in range(2)]
        sel16 = sa("sel16", [P, NT * E], F16)
        pick = [sa(f"pick{i}", [P, NT * E]) for i in range(2)]
        val = [sa(f"val{i}", [P, NT]) for i in range(2)]
        diff = sa("diff", [P, NT])
        ediff = sa("ediff", [P, NT])
        den = sa("den", [P, NT])
        gate = [sa(f"gate{i}", [P, NT]) for i in range(2)]
        pos = sa("pos", [P, NT * E])
        slot_f = sa("slot_f", [P, 2, NT])
        tok = sa("tok", [P, NT])
        w_in = sa("w_in", [P, HC * W])
        w_hi = sa("w_hi", [P, HC * W], F16)
        w_lo = sa("w_lo", [P, HC * W], F16)

        ps = ctx.enter_context(nc.psum_tensor("ps", [P, 8, T], F32))
        max_bank = [ps[:, i, :] for i in range(3)]
        exp_bank = [ps[:, 3 + i, :] for i in range(3)]
        pv_bank = ps[:, 6, :]
        misc_bank = ps[:, 7, :]
        misc16 = misc_bank.bitcast(F16)

        s_con = sem("s_con")
        s_small = sem("s_small")
        s_cst = sem("s_cst")
        s_zero = sem("s_zero")
        s_zq = sem("s_zq")
        s_xin, s_kin, s_vin, s_xres_ld = sem("s_xin"), sem("s_kin"), sem("s_vin"), sem("s_xres_ld")
        s_qh, s_kh = sem("s_qh"), sem("s_kh")
        s_ql, s_kl = sem("s_ql"), sem("s_kl")
        s_qd, s_kd = sem("s_qd"), sem("s_kd")
        s_stk = [sem(f"s_stk{g}") for g in range(4)]
        s_mrow = [sem(f"s_mrow{g}") for g in range(4)]
        s_a = sem("s_a")
        s_red = sem("s_red")
        s_neg = sem("s_neg")
        s_b = sem("s_b")
        s_exp = sem("s_exp")
        s_vx = sem("s_vx")
        s_pv = sem("s_pv")
        s_hd = sem("s_hd")
        s_mw, s_mr = sem("s_mw"), sem("s_mr")
        s_rec = sem("s_rec")
        s_xres = sem("s_xres")
        s_rstd, s_rstd2 = sem("s_rstd"), sem("s_rstd2")
        s_x2st = sem("s_x2st")
        s_zh, s_zl = sem("s_zh"), sem("s_zl")
        s_whi = sem("s_whi")
        s_zcp = sem("s_zcp")
        s_ed = sem("s_ed")
        s_sc = sem("s_sc")
        s_wld, s_wop, s_wst = sem("s_wld"), sem("s_wop"), sem("s_wst")
        s_prep, s_ln2, s_route = sem("s_prep"), sem("s_ln2"), sem("s_route")
        prep = Chain(s_prep, K_PREP)
        ln2 = Chain(s_ln2, K_LN2)
        route = Chain(s_route, K_ROUTE)
        s_pad = sem("s_pad")
        s_held = [sem(f"s_held{i}") for i in range(4)]
        s_tab = sem("s_tab")

        out_v = out[0:TOKENS, :].rearrange("(b i p) c -> b p i c", p=P, i=NT)

        def scatter(pool, b):
            pool.wait_ge(s_route, (b + 1) * K_ROUTE)
            pool.wait_ge(s_zcp, b + 1)
            hold(pool, s_held[2])
            for c in range(2):
                for i in range(NT):
                    nc.gpsimd.indirect_dma_start(
                        out=z_dram, out_offset=bass.IndirectOffsetOnAxis(ap=slot_u[:, c, i:i + 1], axis=0),
                        in_=z_row[c][:, i, :], in_offset=None).then_inc(s_sc, 16)

        attention = ExitStack()
        block = attention.enter_context(nc.Block())

        @block.sync
        def _(sp):
            sp.dma_start(x_in[:, :, :], xq_l[0]).then_inc(s_xin, 16)
            sp.dma_start(con[:, :], const).then_inc(s_con, 16)
            sp.dma_start(kt_in[:, :, :], kT_l[0]).then_inc(s_kin, 16)
            sp.dma_start(bias_sb[:, :], bias.partition_broadcast(P)).then_inc(s_small, 16)
            sp.dma_start(wp_sb[:, :, :], wp_l).then_inc(s_small, 16)
            sp.dma_start(wg_sb[:, :, :], wg_l).then_inc(s_small, 16)
            sp.wait_ge(s_zero, 3)
            for r in range(2):
                for par in range(2):
                    sp.dma_start(q_dram[r, par, :, STACK, :], k_stack[0][0:PAIRS, 0, :]).then_inc(s_zq, 16)

            def load_stacks(it, lag, g):
                b, r = it.it + lag, it.par(lag)
                if it.kind + lag < 2 and g == 0:
                    sp.wait_ge(s_cst, 12 if it.kind + lag else 7)
                if g == 0:
                    sp.wait_ge(s_kd, (b + 1) * 96)
                    sp.wait_ge(s_qd, (b + 1) * 96)
                if it.kind + lag >= 2:
                    sp.wait_ge(s_b, (b - 2) * 64 + 16 * (g + 1))
                for par in range(2):
                    lo = 64 * par
                    sp.dma_start(k_stack[r][lo:lo + STACK, 2 * g:2 * g + 2, :],
                                 k_dram[r, par, 2 * g:2 * g + 2].rearrange("a r t -> r a t")).then_inc(s_stk[g], 16)
                    sp.dma_start(q_stack[r][lo:lo + QROWS, 4 * g + par:4 * g + 4:2, :],
                                 q_dram[r, par, 2 * g:2 * g + 2].rearrange("a r t -> r a t")).then_inc(s_stk[g], 16)

            def load_max(it, lag, g):
                b, r = it.it + lag, it.par(lag)
                sp.wait_ge(s_mr, it.use(lag, "max", g) + 1)
                for n in range(4):
                    par, pl = n // 2, n % 2
                    row = 64 * par + STACK
                    sp.dma_start(q_stack[r][row:row + 1, 4 * g + 2 * pl + par, :],
                                 max_row[g % 2][n:n + 1, :]).then_inc(s_mrow[g], 16)

            def body(it):
                if it.kind == 0:
                    sp.wait_ge(s_cst, 10)
                    sp.dma_start(out[TOKENS:TOKENS + SLOTS, :].rearrange("(s p) c -> p s c", p=P),
                                 fill[:, :, 0:W]).then_inc(s_pad, 16)
                    sp.dma_start(z_dram[E * REGION:E * REGION + SLOTS, :].rearrange("(s p) c -> p s c", p=P),
                                 fill[:, :, :]).then_inc(s_pad, 16)
                if it.has(2) and it.kind + 2 >= 1:
                    b = it.it + 2
                    sp.wait_ge(s_kl, b)
                    sp.wait_ge(s_ql, b)
                    sp.dma_start(x_in[:, :, :], xq_l[at(b)].squeeze(0)).then_inc(s_xin, 16)
                    sp.dma_start(kt_in[:, :, :], kT_l[at(b)].squeeze(0)).then_inc(s_kin, 16)
                if it.has(1):
                    b = it.it + 1
                    ge(sp, s_vx, b)
                    sp.dma_start(v_in[:, :, :], v_l[at(b)].squeeze(0)).then_inc(s_vin, 16)
                if it.has(-1):
                    b = it.it - 1
                    if it.kind - 1 >= 1:
                        sp.wait_ge(s_mr, it.use(-2, "project", 1) + 1)
                    sp.dma_start(x_res[:, :, :], x_l[at(b)].squeeze(0)).then_inc(s_xres_ld, 16)
                if it.has(1):
                    load_stacks(it, 1, 3)
                if it.has(0):
                    load_max(it, 0, 3)
                if it.has(2):
                    b, r = it.it + 2, it.par(2)
                    sp.wait_ge(s_kl, b + 1)
                    for j, part in enumerate((0, 1, 0)):
                        for par in range(2):
                            sp.dma_start(k_dram[r, par, :, j * D:(j + 1) * D, :],
                                         k16[part][:, par, :]).then_inc(s_kd, 16)
                if it.has(1):
                    load_max(it, 1, 0)
                    load_max(it, 1, 1)
                if it.has(-1):
                    b = it.it - 1
                    sp.wait_ge(s_mr, it.use(-1, "project", 1) + 1)
                    hold(sp, s_held[3])
                    if it.kind - 1 >= 1:
                        sp.wait_ge(s_x2st, b * 16)
                    sp.dma_start(out_v[at(b)].squeeze(0), x2[:, :, :]).then_inc(s_x2st, 16)
                if it.has(2):
                    b, r = it.it + 2, it.par(2)
                    sp.wait_ge(s_mr, it.use(2, "turn_q", 1) + 1)
                    if it.kind == FIRST:
                        sp.wait_ge(s_zq, 64)
                    for j, part in enumerate((0, 0, 1)):
                        for par in range(2):
                            sp.dma_start(q_dram[r, par, :, j * D:(j + 1) * D, :],
                                         qt16[part][:, par, :]).then_inc(s_qd, 16)
                    for g in range(3):
                        load_stacks(it, 2, g)
                if it.has(1):
                    load_max(it, 1, 2)

            iterations(sp, body)
            sp.wait_ge(s_x2st, 16 * B)
            sp.wait_ge(s_pad, 32)

        @block.gpsimd
        def _(pool):
            nc.gpsimd.memset(scale_w[:, :], WSCALE).then_inc(s_zero, 1)
            nc.gpsimd.memset(ones16[:, :], 1.0).then_inc(s_zero, 1)
            nc.gpsimd.memset(k_stack[0][:, :, :].bitcast(F32), 0.0).then_inc(s_zero, 1)
            pool.wait_ge(s_zero, 3)

            def prepare():
                nc.gpsimd.memset(k_stack[1][:, :, :].bitcast(F32), 0.0).then_inc(s_zero, 1)
                for i in range(2):
                    nc.gpsimd.memset(v_ext[i][:, :, :, :], 0.0).then_inc(s_zero, 1)
                pool.wait_ge(s_zero, 6)
                for i in range(2):
                    nc.gpsimd.memset(v_ext[i][:, :, :, D:D + 1], 1.0).then_inc(s_zero, 1)
                pool.wait_ge(s_zero, 8)
                pool.wait_ge(s_small, 48)

            def inverse_root(agg, rs, done, b):
                nc.gpsimd.tensor_tensor(rs[:, :], agg[:, :, 1], con[:, C_EPS:C_EPS + 1].to_broadcast([P, NT]),
                                        ALU.add).then_inc(done, 1)
                pool.wait_ge(done, b * 2 + 1)
                nc.gpsimd.tensor_tensor(rs[:, :], rs[:, :], con[:, C_POW:C_POW + 1].to_broadcast([P, NT]),
                                        ALU.pow).then_inc(done, 1)

            def load_weights(n, e, c):
                size = UP if c < 2 else HC * W
                src = w12_l[at(e), c].squeeze(0) if c < 2 else w3_l[at(e)].squeeze(0)
                pool.dma_start(w_in[:, 0:size], src).then_inc(s_wld, 16)

            def split_weights(e, c, more):
                n = e * 3 + c
                size = UP if c < 2 else HC * W
                dst = w12_dram[at(e), :, c] if c < 2 else w3_dram[at(e)]
                x, hi, lo = w_in[:, 0:size], w_hi[:, 0:size], w_lo[:, 0:size]
                pool.wait_ge(s_whi, n + 1)
                nc.gpsimd.tensor_tensor(x, x, scale_w[:, 0:1].to_broadcast([P, size]),
                                        ALU.mult).then_inc(s_wop, 1)
                pool.wait_ge(s_wop, n * 2 + 1)
                nc.gpsimd.tensor_tensor(lo, x, hi, ALU.subtract).then_inc(s_wop, 1)
                pool.wait_ge(s_wop, n * 2 + 2)
                for part, y in enumerate((hi, lo)):
                    pool.dma_start(dst[:, :, part].squeeze(0), y).then_inc(s_wst, 16)
                if more:
                    load_weights(n + 1, e if c < 2 else e + 1, (c + 1) % 3)

            load_weights(0, 0, 0)
            pool.wait_ge(s_con, 16)

            def body(it):
                if it.has(-1):
                    b = it.it - 1
                    pool.wait_ge(s_xres_ld, (b + 1) * 16)
                    xb = x_res[:, :, :]
                    nc.gpsimd.tensor_tensor(xb, xb, bias_sb[:, :].unsqueeze(1).broadcast_to([P, NT, W]),
                                            ALU.add).then_inc(s_xres, 1)
                if it.has(1):
                    b, r = it.it + 1, it.par(1)
                    pool.wait_ge(s_vin, (b + 1) * 16)
                    if it.kind + 1 >= 2:
                        pool.wait_ge(s_pv, (b - 1) * 4)
                    v = v_in[:, :, :].rearrange("p i (h d) -> p i h d", h=H)
                    one = con[:, C_ONE:C_ONE + 1].unsqueeze(2).unsqueeze(3).broadcast_to([P, NT, H, D])
                    nc.gpsimd.tensor_tensor(v_ext[r][:, :, :, 0:D], v, one, ALU.mult).then_inc(s_vx, 1)
                if it.has(2):
                    pool.wait_ge(s_prep, (it.it + 2) * K_PREP + PREP_STAT)
                    inverse_root(mv, rstd, s_rstd, it.it + 2)
                if it.has(1):
                    split_weights(it.it + 1, 0, True)
                if it.has(2):
                    pool.wait_ge(s_kh, it.it + 3)
                    nc.gpsimd.tensor_tensor(k16[1][:, :, :], kt_in[:, :, :], k16[0][:, :, :],
                                            ALU.subtract).then_inc(s_kl, 1)
                if it.has(-2) and it.kind < LAST:
                    scatter(pool, it.it - 2)
                if it.has(2):
                    pool.wait_ge(s_qh, it.it + 3)
                    nc.gpsimd.tensor_tensor(q16[1][:, :, :], x_in[:, :, :], q16[0][:, :, :],
                                            ALU.subtract).then_inc(s_ql, 1)
                if it.has(-1):
                    pool.wait_ge(s_ln2, (it.it - 1) * K_LN2 + LN2_STAT)
                    inverse_root(mv2, rstd2, s_rstd2, it.it - 1)
                if it.has(1):
                    split_weights(it.it + 1, 1, True)
                if it.has(-1):
                    b = it.it - 1
                    pool.wait_ge(s_zh, b + 1)
                    nc.gpsimd.tensor_tensor(z_row[0][:, :, W // 2:W].bitcast(F16), x2[:, :, :],
                                            z_row[0][:, :, 0:W // 2].bitcast(F16), ALU.subtract).then_inc(s_zl, 1)
                    pool.wait_ge(s_zl, b + 1)
                    hold(pool, s_held[2])
                    nc.gpsimd.tensor_copy(z_row[1][:, :, 0:W], z_row[0][:, :, 0:W]).then_inc(s_zcp, 1)
                if it.has(1):
                    split_weights(it.it + 1, 2, it.kind + 1 < B - 1)

            iterations(pool, body, prepare)
            pool.wait_ge(s_wst, 32 * 3 * E)

        @block.scalar
        def _(act):
            act.wait_ge(s_con, 16)

            def high_weights(it, c):
                n = (it.it + 1) * 3 + c
                size = UP if c < 2 else HC * W
                act.wait_ge(s_wld, (n + 1) * 16)
                if it.kind + 1 >= 1 or c:
                    act.wait_ge(s_wst, n * 32)
                nc.scalar.activation(w_hi[:, 0:size], w_in[:, 0:size], ACT.Copy,
                                     scale=WSCALE).then_inc(s_whi, 1)

            def exponentials(it, s, k):
                if not it.has(0):
                    return
                b, g, j, i = it.it, s // 4, s % 4, 4 * s + k
                act.wait_ge(s_b, b * 64 + (i + 1))
                if j == 0 and k == 0 and it.kind * 4 + g >= 2:
                    act.wait_ge(s_pv, b * 4 + (g - 1))
                nc.scalar.activation(probs[g % 2][:, j, k, :], exp_bank[bank_of(i)], ACT.Exp,
                                     scale=0.25).then_inc(s_exp, 1)

            def misc(it, half_slot):
                for m, name, i, lag in it.misc(half_slot):
                    b = it.it + lag
                    if name not in ("max", "turn", "turn_q", "turn_z", "logits"):
                        continue
                    act.wait_ge(s_mw, m + 1)
                    if name == "max":
                        if (it.kind + lag) * 4 + i >= 2:
                            act.wait_ge(s_mrow[(i + 2) % 4], (b if i < 2 else b + 1) * 64)
                        nc.scalar.copy(max_row[i % 2][:, :], misc16[0:4, 0:T]).then_inc(s_mr, 1)
                    if name in ("turn", "turn_z"):
                        nc.scalar.copy(o_t[:, i, :], misc_bank).then_inc(s_mr, 1)
                    if name == "turn_q":
                        if it.kind + lag >= 1:
                            act.wait_ge(s_qd, b * 96)
                        nc.scalar.copy(qt16[i][:, :, :].rearrange("p a t -> p (a t)"), misc16).then_inc(s_mr, 1)
                    if name == "logits":
                        nc.scalar.copy(logit_t[:, :], misc_bank[0:E, :]).then_inc(s_mr, 1)

            def body(it):
                for s in range(H):
                    g, j = s // 4, s % 4
                    exponentials(it, s, 0)
                    exponentials(it, s, 1)
                    misc(it, 2 * s)
                    exponentials(it, s, 2)
                    exponentials(it, s, 3)
                    if j == 3 and (it.has(0) and g >= 1 or g == 0 and it.has(-1)):
                        q = it.it * 4 + g - 1
                        act.wait_ge(s_pv, q + 1)
                        if it.kind * 4 + g - 1 >= 2:
                            lag, i = ((-1, 1), (-1, 2), (-1, 3), (0, 0))[g]
                            act.wait_ge(s_mw, it.use(lag, "heads", i) + 1)
                        nc.scalar.copy(heads[(g - 1) % 2][:, :], pv_bank).then_inc(s_hd, 1)
                    if s in (3, 9, 14) and it.has(1):
                        high_weights(it, (3, 9, 14).index(s))
                    if s == 1 and it.has(-2):
                        act.wait_ge(s_route, (it.it - 2) * K_ROUTE + ROUTE_D)
                        nc.scalar.activation(ediff[:, :], diff[:, :], ACT.Exp).then_inc(s_ed, 1)
                    if s == 2 and it.has(2):
                        b = it.it + 2
                        act.wait_ge(s_kin, (b + 1) * 16)
                        if it.kind + 2 >= 1:
                            act.wait_ge(s_kd, b * 96)
                        nc.scalar.copy(k16[0][:, :, :], kt_in[:, :, :]).then_inc(s_kh, 1)
                    if s == 7 and it.has(2):
                        b = it.it + 2
                        act.wait_ge(s_prep, (b + 1) * K_PREP)
                        if it.kind + 2 >= 1:
                            act.wait_ge(s_mw, it.use(1, "turn_q", 1) + 1)
                        nc.scalar.copy(q16[0][:, :, :], x_in[:, :, :]).then_inc(s_qh, 1)
                    if s == 13 and it.has(-1):
                        b = it.it - 1
                        act.wait_ge(s_ln2, (b + 1) * K_LN2)
                        if it.kind - 1 >= 1:
                            act.wait_ge(s_sc, b * 128)
                        nc.scalar.copy(z_row[0][:, :, 0:W // 2].bitcast(F16), x2[:, :, :]).then_inc(s_zh, 1)
                    misc(it, 2 * s + 1)

            iterations(act, body)

        @block.vector
        def _(dve):
            nc.vector.memset(q_stack[0][:, :, :].bitcast(F32), 0.0).then_inc(s_cst, 1)
            dve.wait_ge(s_con, 16)
            nc.vector.tensor_copy(ident16[:, :], ident).then_inc(s_cst, 1)
            nc.vector.tensor_copy(upper16[:, :], con[:, C_U:C_U + P]).then_inc(s_cst, 1)
            nc.vector.tensor_copy(run[:, :], con[:, C_REG:C_REG + E]).then_inc(s_cst, 1)
            nc.vector.tensor_copy(tok[:, :], con[:, C_TOK:C_TOK + NT]).then_inc(s_cst, 1)
            dve.wait_ge(s_cst, 5)

            def ones_rows(r):
                dve.wait_ge(s_zero, 3 + r)
                for par in range(2):
                    rows = slice(64 * par + 32, 64 * par + 64)
                    nc.vector.tensor_scalar(k_stack[r][rows, :, :], k_stack[r][rows, :, :], 0.0,
                                            con[rows, C_ROW:C_ROW + 1], ALU.mult, ALU.add).then_inc(s_cst, 1)

            def prepare():
                ones_rows(0)
                nc.vector.memset(q_stack[1][:, :, :].bitcast(F32), 0.0).then_inc(s_cst, 1)
                nc.vector.memset(fill[:, :, :], 0.0).then_inc(s_cst, 1)
                dve.wait_ge(s_cst, 9)
                nc.vector.tensor_copy(fill[:, :, W].bitcast(U32), con[:, C_TRASH:C_TRASH + SUB]).then_inc(s_cst, 1)
                ones_rows(1)
                dve.wait_ge(s_cst, 12)

            def take_max(it, s, i):
                if not it.has(1):
                    return
                n = (it.it + 1) * 64 + 4 * s + i
                dve.wait_ge(s_a, n + 1)
                nc.vector.tensor_reduce(mx[it.par(1)][:, i, s:s + 1], max_bank[bank_of(4 * s + i)], AX.X,
                                        ALU.max).then_inc(s_red, 1)

            def norm_step(chain, n, src, st, agg, rs):
                if n < NT:
                    chain.step(nc.vector.bn_stats(st[:, n, :], src[:, n, :]))
                elif n == NT:
                    chain.wait(dve)
                    hold(dve, s_held[0])
                    for i in range(NT):
                        chain.step(nc.vector.bn_aggr(agg[:, i, :], st[:, i, :]))
                else:
                    i = n - NT - 1
                    chain.step(nc.vector.tensor_scalar(src[:, i, :], src[:, i, :], agg[:, i, 0:1],
                                                       rs[:, i:i + 1], ALU.subtract, ALU.mult))

            def prep_step(it, n):
                if not it.has(2):
                    return
                b = it.it + 2
                if n == 0:
                    prep.start(b)
                    dve.wait_ge(s_xin, (b + 1) * 16)
                if n == NT + 1:
                    dve.wait_ge(s_rstd, (b + 1) * 2)
                norm_step(prep, n, x_in, stats, mv, rstd)

            def ln2_step(it, n):
                if not it.has(-1):
                    return
                b = it.it - 1
                if n == 0:
                    ln2.start(b)
                    dve.wait_ge(s_mr, it.use(-1, "project", 0) + 1)
                if n == 2:
                    dve.wait_ge(s_mr, it.use(-1, "project", 1) + 1)
                if n == NT + 1:
                    dve.wait_ge(s_rstd2, (b + 1) * 2)
                    dve.wait_ge(s_x2st, (b + 1) * 16)
                norm_step(ln2, n, x2, stats2, mv2, rstd2)

            def route_step(it, n):
                if not it.has(-2):
                    return
                b = it.it - 2
                tt, ts, reduce = nc.vector.tensor_tensor, nc.vector.tensor_scalar, nc.vector.tensor_reduce
                c1 = cmp1[:, :, :].rearrange("p i (e j) -> p i e j", e=E)
                c2 = cmp2[:, :, :].rearrange("p i (e j) -> p i e j", e=E)
                flat = logit[:, :, :].rearrange("p i e -> p (i e)")
                if n == 0:
                    route.start(b)
                    dve.wait_ge(s_mr, it.use(-2, "turn_l", 0) + 1)
                    of_j = logit[:, :, :].unsqueeze(2).broadcast_to([P, NT, E, E])
                    of_e = logit[:, :, :].unsqueeze(3).broadcast_to([P, NT, E, E])
                    route.step(tt(c1, of_j, of_e, ALU.is_gt))
                    route.step(tt(c2, of_j, of_e, ALU.is_equal))
                    return
                if n < 18:
                    route.wait(dve)
                if n == 1:
                    lower = con[:, C_LT:C_LT + E * E].unsqueeze(1).broadcast_to([P, NT, E * E])
                    route.step(tt(cmp2[:, :, :], cmp2[:, :, :], lower, ALU.mult))
                if n == 2:
                    route.step(tt(cmp1[:, :, :], cmp1[:, :, :], cmp2[:, :, :], ALU.add))
                if n == 3:
                    route.step(reduce(rank[:, :].rearrange("p (i e) -> p i e", e=E), c1, AX.X, ALU.add))
                if n == 4:
                    for c in range(2):
                        route.step(ts(hot[c][:, :], rank[:, :], float(c), None, ALU.is_equal))
                    route.step(ts(sel16[:, :], rank[:, :], 2.0, None, ALU.is_lt))
                    assert route.n == ROUTE_SEL
                if n == 5:
                    for c in range(2):
                        route.step(tt(pick[c][:, :], hot[c][:, :], flat, ALU.mult))
                if n == 6:
                    for c in range(2):
                        route.step(reduce(val[c][:, :], pick[c][:, :].rearrange("p (i e) -> p i e", e=E), AX.X,
                                          ALU.add))
                if n == 7:
                    route.step(tt(diff[:, :], val[1][:, :], val[0][:, :], ALU.subtract))
                    assert route.n == ROUTE_D
                if n == 12:
                    dve.wait_ge(s_ed, b + 1)
                    route.step(ts(den[:, :], ediff[:, :], 1.0, None, ALU.add))
                    for c in range(2):
                        route.step(tt(pick[c][:, :], hot[c][:, :], pos[:, :], ALU.mult))
                if n == 13:
                    route.step(nc.vector.reciprocal(gate[0][:, :], den[:, :]))
                    for c in range(2):
                        route.step(reduce(slot_f[:, c, :], pick[c][:, :].rearrange("p (i e) -> p i e", e=E), AX.X,
                                          ALU.add))
                if n == 14:
                    if it.kind - 2 >= 1:
                        dve.wait_ge(s_sc, b * 128)
                    route.step(tt(gate[1][:, :], ediff[:, :], gate[0][:, :], ALU.mult))
                    route.step(nc.vector.tensor_copy(slot_u[:, :, :], slot_f[:, :, :]))
                if n == 15:
                    for c in range(2):
                        route.step(ts(z_row[c][:, :, W + 1], gate[c][:, :], 1.0 / WSCALE, None, ALU.mult))
                if n == 16:
                    for c in range(2):
                        route.step(nc.vector.tensor_copy(z_row[c][:, :, W].bitcast(U32), tok[:, :]))
                if n == 17:
                    route.step(ts(tok[:, :], tok[:, :], float(T), None, ALU.add))
                    assert route.n == K_ROUTE, route.n

            def misc(it, half_slot):
                for m, name, i, lag in it.misc(half_slot):
                    b = it.it + lag
                    if name == "turn_l":
                        dve.wait_ge(s_mw, m + 1)
                        nc.vector.tensor_copy(logit[:, :, :].rearrange("p i e -> p (i e)"),
                                              misc_bank[:, 0:NT * E]).then_inc(s_mr, 1)
                    if name == "prefix":
                        dve.wait_ge(s_mw, m + 1)
                        route.step(nc.vector.tensor_tensor(
                            pos[:, :].rearrange("p (i e) -> p i e", e=E),
                            misc_bank[:, 0:NT * E].rearrange("p (i e) -> p i e", e=E),
                            run[:, :].unsqueeze(1).broadcast_to([P, NT, E]), ALU.add))
                        route.wait(dve)
                        nc.vector.tensor_tensor(run[:, :], run[:, :], misc_bank[:, NT * E:(NT + 1) * E],
                                                ALU.add).then_inc(s_mr, 1)
                        dve.wait_ge(s_mr, m + 1)
                    if name == "heads":
                        dve.wait_ge(s_mw, m + 1)
                        src = misc_bank.rearrange("p (i h c) -> p i h c", i=NT, h=4)
                        nc.vector.reciprocal(recip[:, :, :], src[:, :, :, D]).then_inc(s_rec, 1)
                        dve.wait_ge(s_rec, b * 4 + (i + 1))
                        nc.vector.tensor_tensor(
                            o_norm[:, :, 64 * i:64 * i + 64].rearrange("p i (h d) -> p i h d", h=4),
                            src[:, :, :, 0:D], recip[:, :, :].unsqueeze(3).broadcast_to([P, NT, 4, D]),
                            ALU.mult).then_inc(s_mr, 1)
                    if name == "project":
                        dve.wait_ge(s_mw, m + 1)
                        dve.wait_ge(s_xres, b + 1)
                        if it.kind + lag >= 1:
                            dve.wait_ge(s_x2st, b * 16)
                            dve.wait_ge(s_zl, b)
                        nc.vector.tensor_tensor(x2[:, 2 * i:2 * i + 2, :],
                                                misc_bank.rearrange("p (i c) -> p i c", i=2),
                                                x_res[:, 2 * i:2 * i + 2, :], ALU.add).then_inc(s_mr, 1)

            def small_step(it, n):
                if n < 18:
                    route_step(it, n)
                if 7 <= n < 7 + NT + 1:
                    prep_step(it, n - 7)
                if 25 <= n < 25 + NT:
                    prep_step(it, n - 25 + NT + 1)
                if 31 <= n < 31 + NT + 1:
                    ln2_step(it, n - 31)
                if 41 <= n < 41 + NT:
                    ln2_step(it, n - 41 + NT + 1)

            def body(it):
                for s in range(H):
                    g, j = s // 4, s % 4
                    take_max(it, s, 0)
                    small_step(it, NT * s)
                    take_max(it, s, 1)
                    small_step(it, NT * s + 1)
                    misc(it, 2 * s)
                    take_max(it, s, 2)
                    small_step(it, NT * s + 2)
                    take_max(it, s, 3)
                    small_step(it, NT * s + 3)
                    if j == 3 and it.has(1):
                        b, r = it.it + 1, it.par(1)
                        dve.wait_ge(s_red, (b * 64) + 16 * (g + 1))
                        if (it.kind + 1) * 4 + g >= 1:
                            dve.wait_ge(s_mw, (it.use(0, "max", 3) if g == 0 else it.use(1, "max", g - 1)) + 1)
                        nc.vector.tensor_scalar(
                            neg_max[:, :, :].rearrange("p i (a b) -> p i a b", a=2),
                            mx[r][:, :, 4 * g:4 * g + 4].rearrange("p i (b a) -> p i a b", a=2),
                            -1.0, None, ALU.mult).then_inc(s_neg, 1)
                    misc(it, 2 * s + 1)

            iterations(dve, body, prepare)

        @block.tensor
        def _(pe):
            pe.wait_ge(s_cst, 2)

            def prepare():
                pe.wait_ge(s_cst, 7)
                pe.wait_ge(s_small, 48)
                pe.wait_ge(s_zero, 8)

            def scores_ts(it, s, i):
                if not it.has(1):
                    return
                b, r, m = it.it + 1, it.par(1), 4 * s + i
                if i == 0 and s % 4 == 0:
                    pe.wait_ge(s_stk[s // 4], (b + 1) * 64)
                if it.kind + 1 >= 1 or m >= 3:
                    pe.wait_ge(s_red, b * 64 + (m - uses_back(m) + 1))
                nc.tensor.matmul(max_bank[bank_of(m)], q_stack[r][:, s, i * P:(i + 1) * P],
                                 k_stack[r][:, s // 2, :], start=True, stop=True).then_inc(s_a, 1)

            def scores_st(it, s, k):
                if not it.has(0):
                    return
                b, r, m = it.it, it.par(), 4 * s + k
                if s % 4 == 0 and k == 0:
                    pe.wait_ge(s_mrow[s // 4], (b + 1) * 64)
                if it.kind >= 1 or m >= 3:
                    pe.wait_ge(s_exp, b * 64 + (m - uses_back(m) + 1))
                nc.tensor.matmul(exp_bank[bank_of(m)], k_stack[r][:, s // 2, k * P:(k + 1) * P],
                                 q_stack[r][:, s, :], start=True, stop=True).then_inc(s_b, 1)

            def weigh(it, g, j, n):
                if not (it.has(0) and g >= 1 or g == 0 and it.has(-1)):
                    return
                q = it.it * 4 + g - 1
                gq, r = (g - 1) % 4, it.par() if g else it.par(-1)
                if j == 0 and n == 0:
                    pe.wait_ge(s_exp, q * 16 + 16)
                    if it.kind * 4 + g - 1 >= 1:
                        pe.wait_ge(s_hd, q)
                    if gq == 0:
                        pe.wait_ge(s_vx, it.it + 1)
                mm = nc.tensor.matmul(pv_bank[32 * n:32 * n + 32, :], v_ext[r][:, j, 4 * gq + n, :],
                                      probs[gq % 2][:, n, j, :], start=(j == 0), stop=(j == NT - 1),
                                      tile_position=(0, 32 * n))
                if j == NT - 1 and n == 3:
                    mm.then_inc(s_pv, 1)

            def misc(it, half_slot):
                for m, name, i, lag in it.misc(half_slot):
                    b = it.it + lag
                    ge(pe, s_mr, m)
                    if name == "turn_l":
                        hold(pe, s_held[1])
                    if name == "max":
                        pe.wait_ge(s_neg, b * 4 + (i + 1))
                        for t in range(NT):
                            mm = nc.tensor.transpose(misc16[0:4, t * P:(t + 1) * P], neg_max[:, t, :], ident16[:, :])
                    if name == "heads":
                        pe.wait_ge(s_hd, b * 4 + (i + 1))
                        for t in range(NT):
                            mm = nc.tensor.transpose(misc_bank[:, t * P:(t + 1) * P],
                                                     heads[i % 2][:, t * P:(t + 1) * P], ident)
                    if name == "turn":
                        for t in range(NT):
                            mm = nc.tensor.transpose(misc_bank[:, t * P:(t + 1) * P],
                                                     o_norm[:, t, i * P:(i + 1) * P], ident)
                    if name == "project":
                        for t in range(2):
                            for k in range(2):
                                tt = 2 * i + t
                                mm = nc.tensor.matmul(misc_bank[:, t * W:(t + 1) * W],
                                                      o_t[:, k, tt * P:(tt + 1) * P], wp_sb[:, k, :],
                                                      start=(k == 0), stop=(k == 1))
                    if name == "turn_q":
                        pe.wait_ge(s_ql if i else s_qh, b + 1)
                        for a in range(2):
                            for t in range(NT):
                                mm = nc.tensor.transpose(misc16[:, a * T + t * P:a * T + (t + 1) * P],
                                                         q16[i][:, t, a * P:(a + 1) * P], ident16[:, :])
                    if name == "turn_z":
                        pe.wait_ge(s_ln2, b * K_LN2 + LN2_Z)
                        for t in range(NT):
                            mm = nc.tensor.transpose(misc_bank[:, t * P:(t + 1) * P],
                                                     x2[:, t, i * P:(i + 1) * P], ident)
                    if name == "logits":
                        for k in range(2):
                            mm = nc.tensor.matmul(misc_bank[0:E, :], wg_sb[:, k, :], o_t[:, k, :],
                                                  start=(k == 0), stop=(k == 1))
                    if name == "turn_l":
                        for t in range(NT):
                            mm = nc.tensor.transpose(misc_bank[:, t * E:(t + 1) * E],
                                                     logit_t[:, t * P:(t + 1) * P], ident[0:E, 0:E])
                    if name == "prefix":
                        pe.wait_ge(s_route, b * K_ROUTE + ROUTE_SEL)
                        nc.tensor.matmul(misc_bank[:, 0:NT * E], upper16[:, :], sel16[:, :], start=True,
                                         stop=False, skip_group_check=True)
                        for t in range(1, NT + 1):
                            for t0 in range(t):
                                mm = nc.tensor.matmul(misc_bank[:, t * E:(t + 1) * E], ones16[:, :],
                                                      sel16[:, t0 * E:(t0 + 1) * E], start=False,
                                                      stop=(t == NT and t0 == t - 1), skip_group_check=True)
                    mm.then_inc(s_mw, 1)

            def body(it):
                for s in range(H):
                    g, j = s // 4, s % 4
                    scores_st(it, s, 0)
                    scores_ts(it, s, 0)
                    scores_st(it, s, 1)
                    weigh(it, g, j, 0)
                    weigh(it, g, j, 1)
                    scores_ts(it, s, 1)
                    misc(it, 2 * s)
                    scores_st(it, s, 2)
                    weigh(it, g, j, 2)
                    scores_ts(it, s, 2)
                    scores_st(it, s, 3)
                    scores_ts(it, s, 3)
                    weigh(it, g, j, 3)
                    misc(it, 2 * s + 1)

            iterations(pe, body, prepare)

        attention.close()
        att.close()

        with ExitStack() as ffn:
            def sf(name, shape, dt=F32):
                return ffn.enter_context(nc.sbuf_tensor(name, shape, dt))

            cnt = sf("cnt", [P, E])
            cmp3 = sf("cmp3", [P, E, NCNT])
            n_tiles = sf("n_tiles", [P, E])
            cmp4 = sf("cmp4", [P, E, E])
            t_end = sf("t_end", [P, E])
            t_begin = sf("t_begin", [P, E])
            origin = sf("origin", [P, E])
            cmp5 = sf("cmp5", [P, FFN_TILES, E])
            cmp6 = sf("cmp6", [P, FFN_TILES, E])
            expert = sf("expert", [P, FFN_TILES])
            row_f = sf("row_f", [P, FFN_TILES])
            row_tab = sf("row_tab", [P, FFN_TILES], I32)
            exp_tab = sf("exp_tab", [P, FFN_TILES], I32)
            new_tab = sf("new_tab", [P, FFN_TILES], I32)
            tot_tab = sf("tot_tab", [P, 1], I32)
            pad_tab = sf("pad_tab", [P, E], I32)
            z_in = [sf(f"z_in{i}", [P, SUB, ROW]) for i in range(2)]
            aim = [sf(f"aim{i}", [P, SUB, 2]) for i in range(2)]
            w12 = [sf(f"w12_{i}", [P, 2, 2, UP], F16) for i in range(2)]
            w3 = [sf(f"w3_{i}", [P, 2, HC, W], F16) for i in range(2)]
            zt16 = [sf(f"zt16_{i}", [P, 2, 2, SLOTS], F16) for i in range(2)]
            silu = [sf(f"silu{i}", [P, SLOTS]) for i in range(2)]
            hid = [sf(f"hid{i}", [P, SLOTS]) for i in range(2)]
            hid16 = sf("hid16", [P, FULL, 2, SLOTS], F16)
            tail16 = sf("tail16", [P, SLOTS], F16)
            top, upper = slice(0, HALF), slice(HALF, P)
            y = [sf(f"y{i}", [P, SUB, W]) for i in range(2)]
            y_bank = [ps[:, 4, 0:W], ps[:, 5, 0:W]]
            turn16 = ps[:, 6, :].bitcast(F16)

            f_pad = sem("f_pad")
            f_z = [sem("f_z0"), sem("f_z1")]
            f_w = [sem("f_w0"), sem("f_w1")]
            f_aim = sem("f_aim")
            f_turn = sem("f_turn")
            f_zt = sem("f_zt")
            f_up = sem("f_up")
            f_silu = sem("f_silu")
            f_hid = sem("f_hid")
            f_hi, f_lo = sem("f_hi"), sem("f_lo")
            f_down = sem("f_down")
            f_y = sem("f_y")
            f_add = sem("f_add")
            K_TAB = 20

            def tiles_in_use(eng):
                eng.wait_ge(s_tab, K_TAB)
                return eng.value_load(tot_tab[0:1, 0:1], min_val=FIRM_TILES, max_val=FFN_TILES)


            block2 = ffn.enter_context(nc.Block())

            @block2.vector
            def _(dve):
                n = 0

                def step(ins):
                    nonlocal n
                    n += 1
                    ins.then_inc(s_tab, 1)
                    dve.wait_ge(s_tab, n)

                reg = con[:, C_REG:C_REG + E]
                tt = nc.vector.tensor_tensor
                step(nc.vector.tensor_copy(pad_tab[:, :], run[:, :]))
                step(tt(cnt[:, :], run[:, :], reg, ALU.subtract))
                step(tt(cmp3[:, :, :], cnt[:, :].unsqueeze(2).broadcast_to([P, E, NCNT]),
                        con[:, C_CNT:C_CNT + NCNT].unsqueeze(1).broadcast_to([P, E, NCNT]), ALU.is_gt))
                step(nc.vector.tensor_reduce(n_tiles[:, :], cmp3[:, :, :], AX.X, ALU.add))
                step(tt(cmp4[:, :, :], con[:, C_LE:C_LE + E * E].rearrange("p (e j) -> p e j", e=E),
                        n_tiles[:, :].unsqueeze(1).broadcast_to([P, E, E]), ALU.mult))
                step(nc.vector.tensor_reduce(t_end[:, :], cmp4[:, :, :], AX.X, ALU.add))
                step(tt(t_begin[:, :], t_end[:, :], n_tiles[:, :], ALU.subtract))
                step(nc.vector.scalar_tensor_tensor(out=origin[:, :], in0=t_begin[:, :], scalar=-float(SLOTS),
                                                    in1=reg, op0=ALU.mult, op1=ALU.add))
                big = [P, FFN_TILES, E]
                step(tt(cmp5[:, :, :], t_end[:, :].unsqueeze(1).broadcast_to(big),
                        con[:, C_K:C_K + FFN_TILES].unsqueeze(2).broadcast_to(big), ALU.is_le))
                step(nc.vector.tensor_reduce(expert[:, :], cmp5[:, :, :], AX.X, ALU.add))
                step(tt(cmp5[:, :, :], expert[:, :].unsqueeze(2).broadcast_to(big),
                        con[:, C_E:C_E + E].unsqueeze(1).broadcast_to(big), ALU.is_equal))
                step(tt(cmp6[:, :, :], origin[:, :].unsqueeze(1).broadcast_to(big),
                        con[:, C_KS:C_KS + FFN_TILES].unsqueeze(2).broadcast_to(big), ALU.add))
                step(tt(cmp5[:, :, :], cmp5[:, :, :], cmp6[:, :, :], ALU.mult))
                step(nc.vector.tensor_reduce(row_f[:, :], cmp5[:, :, :], AX.X, ALU.add))
                step(nc.vector.tensor_scalar(row_tab[:, :], row_f[:, :], float(E * REGION), None, ALU.add))
                step(nc.vector.tensor_scalar(expert[:, :], expert[:, :], float(E - 1), None, ALU.min))
                step(nc.vector.tensor_copy(exp_tab[:, :], expert[:, :]))
                step(nc.vector.memset(new_tab[:, 0:2], 1))
                step(nc.vector.tensor_copy(tot_tab[:, :], t_end[:, E - 1:E]))
                step(tt(new_tab[:, 2:FFN_TILES], expert[:, 2:FFN_TILES], expert[:, 0:FFN_TILES - 2],
                        ALU.not_equal))
                assert n == K_TAB
                total = tiles_in_use(dve)

                def body(k, half, par, least):
                    if least >= 2:
                        dve.wait_ge(f_add, (k - 1) * 32)
                    dve.wait_ge(f_z[par], half * 16 + 16)
                    nc.vector.tensor_copy(aim[par][:, :, :].bitcast(I32),
                                          z_in[par][:, :, W:W + 2].bitcast(I32)).then_inc(f_aim, 1)
                    for m in range(HC + 1):
                        if m < HC:
                            u, bank = k * HC + m, (m + 2 * par) % 4
                            dve.wait_ge(f_silu, u + 1)
                            if least * HC + m >= 2:
                                dve.wait_ge(f_hi, u - 1)
                                dve.wait_ge(f_lo, u - 1)
                            rows = slice(0, P) if m < FULL else upper
                            gated = ps[:, bank, W:2 * W] if m < FULL else ps[upper, bank, 0:W]
                            nc.vector.scalar_tensor_tensor(
                                out=hid[m % 2][rows, :], in0=gated, scalar=1.0 / WSCALE,
                                in1=silu[m % 2][rows, :], op0=ALU.mult, op1=ALU.mult).then_inc(f_hid, 1)
                        if m >= 1:
                            u = k * HC + (m - 1)
                            dve.wait_ge(f_hi, u + 1)
                            if m - 1 < FULL:
                                nc.vector.tensor_tensor(hid16[:, m - 1, 1, :], hid[(m - 1) % 2][:, :],
                                                        hid16[:, m - 1, 0, :], ALU.subtract).then_inc(f_lo, 1)
                            else:
                                nc.vector.tensor_tensor(tail16[top, :], hid[FULL % 2][upper, :],
                                                        tail16[upper, :], ALU.subtract).then_inc(f_lo, 1)
                    dve.wait_ge(f_aim, k + 1)
                    for t in range(SUB):
                        dve.wait_ge(f_down, k * SUB + (t + 1))
                        nc.vector.tensor_scalar(y[par][:, t, :], y_bank[t], aim[par][:, t, 1:2], None,
                                                ALU.mult).then_inc(f_y, 1)

                ffn_tiles(dve, total, (body, 0))

            @block2.scalar
            def _(act):
                def keep_turned(k, par, least):
                    act.wait_ge(f_turn, k + 1)
                    nc.scalar.copy(zt16[par][:, :, :, :].rearrange("p k a s -> p (k a s)"),
                                   turn16).then_inc(f_zt, 1)

                total = tiles_in_use(act)
                keep_turned(0, 0, 0)

                def body(k, half, par, least):
                    for m in range(HC + 1):
                        if m < HC:
                            u, bank = k * HC + m, (m + 2 * par) % 4
                            act.wait_ge(f_up, u + 1)
                            if least * HC + m >= 2:
                                act.wait_ge(f_hid, u - 1)
                            to, rows = (slice(0, P), slice(0, P)) if m < FULL else (upper, top)
                            nc.scalar.activation(silu[m % 2][to, :], ps[rows, bank, 0:W], ACT.Silu,
                                                 scale=1.0 / WSCALE).then_inc(f_silu, 1)
                        if m >= 1:
                            u = k * HC + (m - 1)
                            act.wait_ge(f_hid, u + 1)
                            if least >= 1:
                                act.wait_ge(f_down, k * SUB)
                            if m - 1 < FULL:
                                nc.scalar.copy(hid16[:, m - 1, 0, :], hid[(m - 1) % 2][:, :]).then_inc(f_hi, 1)
                            else:
                                nc.scalar.copy(tail16[upper, :], hid[FULL % 2][upper, :]).then_inc(f_hi, 1)
                    if least < FFN_TILES - 1:
                        keep_turned(k + 1, 1 - par, least + 1)

                ffn_tiles(act, total, (body, 0))

            @block2.tensor
            def _(pe):
                def turn(k, half, par, least):
                    pe.wait_ge(f_z[par], half * 16 + 16)
                    if least >= 1:
                        pe.wait_ge(f_zt, k)
                    rows = z_in[par][:, :, 0:W].bitcast(F16).rearrange("p s (a k c) -> p s a k c", a=2, k=2)
                    for kk in range(2):
                        for a in range(2):
                            for t in range(SUB):
                                col = (kk * 2 + a) * SLOTS + t * P
                                mm = nc.tensor.transpose(turn16[:, col:col + P], rows[:, t, a, kk, :], ident16[:, :])
                    mm.then_inc(f_turn, 1)

                total = tiles_in_use(pe)
                turn(0, 0, 0, 0)

                def body(k, half, par, least):
                    pe.wait_ge(f_zt, k + 1)
                    pe.wait_ge(f_w[par], half * 32 + 32)
                    z16, w = zt16[par], w12[par]
                    for m in range(HC):
                        u, bank = k * HC + m, (m + 2 * par) % 4
                        if least * HC + m >= 4:
                            pe.wait_ge(f_hid, u - 3)
                        for c in range(2 if m < FULL else 1):
                            dst = ps[:, bank, c * W:(c + 1) * W]
                            chunk = c * FULL + m if m < FULL else 2 * FULL
                            cols = slice(chunk * P, (chunk + 1) * P)
                            for kk in range(2):
                                nc.tensor.matmul(dst, w[:, kk, 1, cols], z16[:, kk, 0, :],
                                                 start=(kk == 0), stop=False)
                                nc.tensor.matmul(dst, w[:, kk, 0, cols], z16[:, kk, 1, :],
                                                 start=False, stop=False)
                                mm = nc.tensor.matmul(dst, w[:, kk, 0, cols], z16[:, kk, 0, :],
                                                      start=False, stop=(kk == 1))
                        mm.then_inc(f_up, 1)
                    if least < FFN_TILES - 1:
                        turn(k + 1, half + par, 1 - par, least + 1)
                    if least >= 1:
                        pe.wait_ge(f_y, k * SUB)
                    for m in range(HC):
                        pe.wait_ge(f_lo, k * HC + (m + 1))
                        for t in range(SUB):
                            slots = slice(t * P, (t + 1) * P)
                            if m < FULL:
                                h = [hid16[:, m, a, slots] for a in range(2)]
                                nc.tensor.matmul(y_bank[t], h[1], w3[par][:, 0, m, :], start=(m == 0), stop=False)
                                nc.tensor.matmul(y_bank[t], h[0], w3[par][:, 1, m, :], start=False, stop=False)
                                nc.tensor.matmul(y_bank[t], h[0], w3[par][:, 0, m, :], start=False, stop=False)
                            else:
                                nc.tensor.matmul(y_bank[t], tail16[:, slots], w3[par][:, 1, m, :],
                                                 start=False, stop=False)
                                nc.tensor.matmul(y_bank[t], tail16[:, slots], w3[par][:, 0, m, :],
                                                 start=False, stop=True).then_inc(f_down, 1)

                ffn_tiles(pe, total, (body, 0))

            @block2.sync
            def _(sp):
                def load_expert(k, half, par, least):
                    e = sp.value_load(exp_tab[0:1, at(k)], min_val=0, max_val=E - 1)
                    new = sp.value_load(new_tab[0:1, at(k)], min_val=0, max_val=1)
                    if least >= 2:
                        sp.wait_ge(f_down, (k - 1) * SUB)
                    hold(sp, s_held[3])
                    sp.dma_start(w12[par][:, :, :, :].rearrange("p k a h -> p (k a h)"),
                                 w12_dram[bass.ds(e, 1)].rearrange("o p k a h -> p (o k a h)"), cond=new
                                 ).then_inc(f_w[par], 16)
                    sp.dma_start(w3[par][:, :, :, :].rearrange("p a m c -> p (a m c)"),
                                 w3_dram[bass.ds(e, 1)].rearrange("o p a h -> p (o a h)"), cond=new
                                 ).then_inc(f_w[par], 16)

                sp.wait_ge(s_tab, 1)
                for e in range(E):
                    first = sp.value_load(pad_tab[0:1, e:e + 1], min_val=0, max_val=E * REGION)
                    sp.dma_start(z_dram[bass.ds(first, SLOTS), :].rearrange("(s p) c -> p s c", p=P),
                                 fill[:, :, :]).then_inc(f_pad, 16)
                sp.wait_ge(s_tab, K_TAB)
                total = tiles_in_use(sp)
                load_expert(0, 0, 0, 0)
                sp.wait_ge(f_pad, 16 * E)
                sp.wait_ge(s_sc, 128 * B)

                def load_rows(k, half, par, least):
                    first = sp.value_load(row_tab[0:1, at(k)], min_val=0, max_val=E * REGION)
                    if least >= 2:
                        sp.wait_ge(f_turn, k - 1)
                        sp.wait_ge(f_aim, k - 1)
                    hold(sp, s_held[3])
                    sp.dma_start(z_in[par][:, :, :], z_dram[bass.ds(first, SLOTS), :].rearrange(
                        "(s p) c -> p s c", p=P)).then_inc(f_z[par], 16)

                def load_later(k, half, par, least):
                    if least >= 1:
                        load_expert(k, half, par, least)

                ffn_tiles(sp, total, (load_rows, 1), (load_later, 0))

            @block2.gpsimd
            def _(pool):
                scatter(pool, B - 1)
                total = tiles_in_use(pool)

                def body(k, half, par, least):
                    for t in range(SUB):
                        pool.wait_ge(f_y, k * SUB + (t + 1))
                        if least or t:
                            pool.wait_ge(f_add, (k * SUB + t) * 16)
                        hold(pool, s_held[2])
                        nc.gpsimd.indirect_dma_start(
                            out=out, out_offset=bass.IndirectOffsetOnAxis(ap=aim[par][:, t, 0:1].bitcast(U32), axis=0),
                            in_=y[par][:, t, :], in_offset=None, compute_op=ALU.add).then_inc(f_add, 16)

                ffn_tiles(pool, total, (body, 0))
                pool.wait_ge(f_add, total * (16 * SUB))
                hold(pool, s_held[2])


def kernel(x, ctx_1024, L0_xattn_w_proj, L0_xattn_b_proj, L0_ffn_Wg, L0_ffn_W1, L0_ffn_W2, L0_ffn_W3):
    import numpy as np
    import concourse.bacc as bacc
    from concourse.bass_utils import run_bass_kernel_spmd

    def tiles(a):
        return np.ascontiguousarray(np.asarray(a).reshape(B, NT, P, W).transpose(0, 2, 1, 3))

    c = np.asarray(ctx_1024)
    x_q = np.asarray(x).reshape(B, T, PAIRS, 2, D).transpose(0, 1, 3, 2, 4)
    k_t = c.reshape(B, T, PAIRS, 2, D).transpose(0, 2, 4, 3, 1).reshape(B, P, 2, T)
    w12 = np.zeros((E, 2, P, UP), np.float32)
    for n, w in enumerate((L0_ffn_W1, L0_ffn_W2)):
        w = np.asarray(w).reshape(E, HID, 2, P).transpose(0, 2, 3, 1)
        w12[:, :, :, n * FULL * P:(n + 1) * FULL * P] = w[:, :, :, 0:FULL * P]
        tail = 2 * FULL * P + n * HALF
        w12[:, :, :, tail:tail + HID - FULL * P] = w[:, :, :, FULL * P:HID]
    w = np.asarray(L0_ffn_W3).transpose(0, 2, 1)
    w3 = np.zeros((E, P, HC, W), np.float32)
    w3[:, :, 0:FULL] = w[:, 0:FULL * P].reshape(E, FULL, P, W).transpose(0, 2, 1, 3)
    for half in range(2):
        w3[:, half * HALF:half * HALF + HID - FULL * P, FULL] = w[:, FULL * P:HID]
    w3 = w3.reshape(E, P, HC * W)
    wp = np.asarray(L0_xattn_w_proj).T.reshape(2, P, W).transpose(1, 0, 2)
    wg = np.asarray(L0_ffn_Wg).T.reshape(2, P, E).transpose(1, 0, 2)
    arrays = {"x": tiles(x), "x_q": tiles(x_q), "v": tiles(c), "k_t": k_t, "w_proj": wp, "b_proj": np.asarray(L0_xattn_b_proj),
              "w_gate": wg, "w12": w12, "w3": w3, "const": constants()}
    arrays = {k: np.ascontiguousarray(v) for k, v in arrays.items()}
    nc = bacc.Bacc("TRN2", target_bir_lowering=False, num_devices=1)
    nc.disable_value_cache = True
    d = {k: nc.dram_tensor(f"in_{k}", v.shape, F32, kind="ExternalInput").ap() for k, v in arrays.items()}
    out = nc.dram_tensor("out", (TOKENS + SLOTS, W), F32, kind="ExternalOutput").ap()
    build(nc, d["x_q"], d["x"], d["v"], d["k_t"], d["w_proj"], d["b_proj"], d["w_gate"], d["w12"], d["w3"],
          d["const"], out)
    r = run_bass_kernel_spmd(nc, [{f"in_{k}": v for k, v in arrays.items()}], core_ids=[0])
    return r.results[0]["out"][:TOKENS].reshape(B, T, W)
```
